# Optimizing a Trainium2 kernel written in Bass

```python
import numpy as np
import jax
import jax.numpy as jnp

def _softmax(x, axis=-1):
    return jax.nn.softmax(x, axis=axis)

def _gelu(x):
    return jax.nn.gelu(x, approximate=True)

def _silu(x):
    return jax.nn.silu(x)

def _sigmoid(x):
    return jax.nn.sigmoid(x)

def _layernorm(x, axis=-1, eps=1e-05):
    m = jnp.mean(x, axis=axis, keepdims=True)
    v = jnp.var(x, axis=axis, keepdims=True)
    return (x - m) / jnp.sqrt(v + eps)

def _scatter_add(tgt, idx, src, axis=0):
    return tgt.at[idx].add(src)

def _segment_sum(src, seg, n):
    return jax.ops.segment_sum(src, seg, n)
kernel_name = 'mk_hybrid_d1_jaxref_r8_c6b708'

def setup_inputs(seed: int=0):
    np.random.seed(seed)
    _w = jnp.asarray

    def _L0_attn_a_setup():
        import jax, jax.numpy as jnp
        import numpy as np
        EMBED = 128
        HEADS = 16
        HEAD_DIM = EMBED // HEADS
        WIN = 32
        key = jax.random.key(seed)
        k0, k1, k2 = jax.random.split(key, 3)
        s = 0.02
        return {'x': jax.random.normal(k0, (4, 512, EMBED), dtype=jnp.float32), 'W_qkv': jax.random.normal(k1, (EMBED, 3 * EMBED), dtype=jnp.float32) * s, 'b_qkv': jnp.zeros((3 * EMBED,), dtype=jnp.float32), 'W_out': jax.random.normal(k2, (EMBED, EMBED), dtype=jnp.float32) * s, 'b_out': jnp.zeros((EMBED,), dtype=jnp.float32)}
    _L0_attn_a_in = _L0_attn_a_setup()

    def _L0_attn_b_setup():
        import jax, jax.numpy as jnp
        import numpy as np
        D_MODEL = 128
        NUM_HEADS = 16
        D_K = D_MODEL // NUM_HEADS
        key = jax.random.key(seed)
        k1, k2, k3, k4, k5 = jax.random.split(key, 5)
        scale = 1.0 / np.sqrt(D_MODEL)
        x = jax.random.normal(k1, (2, 1024, D_MODEL), dtype=jnp.float32)
        W_qkv = jax.random.normal(k2, (D_MODEL, 3 * D_MODEL), dtype=jnp.float32) * scale
        b_qkv = jax.random.normal(k3, (3 * D_MODEL,), dtype=jnp.float32) * 0.01
        W_out = jax.random.normal(k4, (D_MODEL, D_MODEL), dtype=jnp.float32) * scale
        b_out = jax.random.normal(k5, (D_MODEL,), dtype=jnp.float32) * 0.01
        return {'x': x, 'W_qkv': W_qkv, 'b_qkv': b_qkv, 'W_out': W_out, 'b_out': b_out}
    _L0_attn_b_in = _L0_attn_b_setup()

    def _L0_ffn_setup():
        import jax, jax.numpy as jnp
        import numpy as np
        N_EMBD = 128
        N_STATE = 512
        key = jax.random.key(seed)
        k_x, k_w1, k_b1, k_w2, k_b2 = jax.random.split(key, 5)
        x = jax.random.normal(k_x, (4, 256, N_EMBD), dtype=jnp.float32)
        w1 = jax.random.normal(k_w1, (N_EMBD, N_STATE), dtype=jnp.float32) * (1.0 / np.sqrt(N_EMBD))
        b1 = jax.random.normal(k_b1, (N_STATE,), dtype=jnp.float32) * 0.02
        w2 = jax.random.normal(k_w2, (N_STATE, N_EMBD), dtype=jnp.float32) * (1.0 / np.sqrt(N_STATE))
        b2 = jax.random.normal(k_b2, (N_EMBD,), dtype=jnp.float32) * 0.02
        return {'x': x, 'w1': w1, 'b1': b1, 'w2': w2, 'b2': b2}
    _L0_ffn_in = _L0_ffn_setup()
    _d = {'L0_attn_a_x': _L0_attn_a_in['x'], 'L0_attn_a_W_qkv': _L0_attn_a_in['W_qkv'], 'L0_attn_a_b_qkv': _L0_attn_a_in['b_qkv'], 'L0_attn_a_W_out': _L0_attn_a_in['W_out'], 'L0_attn_a_b_out': _L0_attn_a_in['b_out'], 'L0_attn_b_W_qkv': _L0_attn_b_in['W_qkv'], 'L0_attn_b_b_qkv': _L0_attn_b_in['b_qkv'], 'L0_attn_b_W_out': _L0_attn_b_in['W_out'], 'L0_attn_b_b_out': _L0_attn_b_in['b_out'], 'L0_ffn_w1': _L0_ffn_in['w1'], 'L0_ffn_b1': _L0_ffn_in['b1'], 'L0_ffn_w2': _L0_ffn_in['w2'], 'L0_ffn_b2': _L0_ffn_in['b2']}
    _x0 = _d['L0_attn_a_x']
    _d['L0_attn_a_x'] = jax.random.normal(jax.random.fold_in(jax.random.key(seed), 1), (2, 1024, 128), dtype=_x0.dtype)
    del _x0
    return _d

def reference(L0_attn_a_x, L0_attn_a_W_qkv, L0_attn_a_b_qkv, L0_attn_a_W_out, L0_attn_a_b_out, L0_attn_b_W_qkv, L0_attn_b_b_qkv, L0_attn_b_W_out, L0_attn_b_b_out, L0_ffn_w1, L0_ffn_b1, L0_ffn_w2, L0_ffn_b2):

    def _L0_attn_a_ref(x, W_qkv, b_qkv, W_out, b_out):
        import jax, jax.numpy as jnp
        import numpy as np
        EMBED = 128
        HEADS = 16
        HEAD_DIM = EMBED // HEADS
        WIN = 32
        B, L, C = x.shape
        pad_l = -L % WIN
        xp = jnp.pad(x, ((0, 0), (0, pad_l), (0, 0)))
        Lp = L + pad_l
        qkv = (xp @ W_qkv + b_qkv).reshape(B, Lp, 3, HEADS, HEAD_DIM)
        qkv = qkv.transpose(2, 0, 3, 1, 4)
        q, k, v = (qkv[0], qkv[1], qkv[2])
        step = WIN // 2
        Nw = (Lp - WIN) // step + 1
        win_idx = jnp.arange(Nw)[:, None] * step + jnp.arange(WIN)[None, :]

        def unfold(a):
            return a[:, :, win_idx, :].transpose(0, 1, 2, 4, 3)
        qw, kw, vw = (unfold(q), unfold(k), unfold(v))
        attn = jnp.einsum('bhndw,bhnew->bhnde', qw, kw) * HEAD_DIM ** (-0.5)
        attn = jax.nn.softmax(attn, axis=-1)
        o = jnp.einsum('bhnde,bhnew->bhndw', attn, vw)
        o = o.reshape(B, HEADS, -1, HEAD_DIM)
        o = o.transpose(0, 2, 1, 3).reshape(B, -1, C)
        o = o[:, :L]
        return o @ W_out + b_out

    def _L0_attn_b_ref(x, W_qkv, b_qkv, W_out, b_out):
        import jax, jax.numpy as jnp
        import numpy as np
        D_MODEL = 128
        NUM_HEADS = 16
        D_K = D_MODEL // NUM_HEADS
        B, S, _ = x.shape
        qkv = (jnp.einsum('bsd,de->bse', x, W_qkv) + b_qkv).reshape(B, S, NUM_HEADS, 3 * D_K)
        q, k, v = (qkv[..., :D_K], qkv[..., D_K:2 * D_K], qkv[..., 2 * D_K:])
        scores = jnp.einsum('bshd,bsgd->bshg', q, k) / np.sqrt(D_K)
        attn = jax.nn.softmax(scores, axis=-1)
        context = jnp.einsum('bshg,bsgd->bshd', attn, v).reshape(B, S, NUM_HEADS * D_K)
        return jnp.einsum('bsd,de->bse', context, W_out) + b_out

    def _L0_ffn_ref(x, w1, b1, w2, b2):
        import jax, jax.numpy as jnp
        import numpy as np
        N_EMBD = 128
        N_STATE = 512
        h = jax.nn.gelu(jnp.einsum('bse,eh->bsh', x, w1) + b1, approximate=False)
        return jnp.einsum('bsh,he->bse', h, w2) + b2
    x = L0_attn_a_x
    x = x + _L0_attn_a_ref(_layernorm(x, axis=-1), L0_attn_a_W_qkv, L0_attn_a_b_qkv, L0_attn_a_W_out, L0_attn_a_b_out)
    x = x + _L0_ffn_ref(_layernorm(x, axis=-1), L0_ffn_w1, L0_ffn_b1, L0_ffn_w2, L0_ffn_b2)
    x = x + _L0_attn_b_ref(_layernorm(x, axis=-1), L0_attn_b_W_qkv, L0_attn_b_b_qkv, L0_attn_b_W_out, L0_attn_b_b_out)
    x = x + _L0_ffn_ref(_layernorm(x, axis=-1), L0_ffn_w1, L0_ffn_b1, L0_ffn_w2, L0_ffn_b2)
    return x

_drawn_inputs = setup_inputs


def setup_inputs(seed=0):
    import zlib

    import numpy as np

    out = dict(_drawn_inputs(seed))
    spreads = {'L0_attn_a_b_qkv': (0.0, 0.8), 'L0_attn_a_b_out': (0.0, 0.1)}
    factors = {'L0_attn_a_W_qkv': 3.085,
     'L0_attn_a_W_out': 2.908,
     'L0_attn_b_b_qkv': 8.0,
     'L0_attn_b_b_out': 8.0,
     'L0_ffn_b1': 3.385}
    for name, (base, spread) in spreads.items():
        noise = np.random.default_rng([zlib.crc32(name.encode()), seed]).standard_normal(out[name].shape)
        drawn = base * np.exp(spread * noise) if base else spread * noise
        out[name] = jnp.asarray(drawn.astype(out[name].dtype))
    for name, factor in factors.items():
        out[name] = (out[name] * factor).astype(out[name].dtype)
    return out
```

```python
from contextlib import ExitStack

import concourse.bass as bass
from concourse import mybir

P = 128
F32 = mybir.dt.float32
BF16 = mybir.dt.bfloat16
ALU = mybir.AluOpType
ACT = mybir.ActivationFunctionType
AX_X = mybir.AxisListType.X

HEADS = 16
HD = 8
WIN = 32
HOP = WIN // 2
EPS = 1e-5
SCALE = float(HD) ** -0.5
QUAD = 32
HQ = QUAD // HD
ROWS_PER_WIN = WIN
NW = P // ROWS_PER_WIN
GROUPS = WIN // HD

STEP = [("b_project", 6), ("b_scores_0", 5), ("b_residual", 6), ("b_scores_1", 5), ("b_softmax", 5),
        ("a_context", 2), ("a_softmax", 1), ("a_front", 0), ("f2_up", 6), ("f1_up", 3), ("b_front", 4),
        ("b_context_0", 5), ("f2_down", 6), ("f1_down", 3), ("a_project", 2), ("b_context_1", 5)]
LAG = max(d for _, d in STEP)


class Tile:

    def __init__(self, n, half):
        self.n, self.half = n, half


def wait(eng, sem, count):
    if isinstance(count, int) and count <= 0:
        return
    eng.wait_ge(sem, count)


def walk(eng, tiles, stages):
    def at(s):
        for name, lag in STEP:
            if name in stages and 0 <= s - lag < tiles:
                stages[name](Tile(s - lag, (s - lag) % 2))

    begin = LAG + 2
    for s in range(begin):
        at(s)
    with eng.Fori(0, (tiles - begin) // 2) as pair:
        for odd in range(2):
            for name, lag in STEP:
                if name in stages:
                    stages[name](Tile(pair * 2 + (begin + odd - lag), (begin + odd - lag) % 2))
    for s in range(begin + (tiles - begin) // 2 * 2, tiles + LAG):
        at(s)


def hybrid_block(nc, x, a_wqkv, a_bqkv, a_wout, a_bout, b_wqkv, b_bqkv, b_wout, b_bout,
                 f_w1, f_b1, f_w2, f_b2, out):
    B, L, C = x.shape
    FF = f_w1.shape[1]
    NF = FF // P
    TPB = L // P
    T = B * TPB
    assert C == P == HEADS * HD and NF * P == 512
    HOP_T = NW * HOP
    assert (L - P) // P * HOP_T + (NW - 1) * HOP + WIN <= L

    with ExitStack() as ctx:
        def sb(name, shape, dt=F32):
            return ctx.enter_context(nc.sbuf_tensor(name, shape, dt))

        def sem(name):
            return ctx.enter_context(nc.semaphore(name))

        xw = sb("xw", [P, T, C])
        xs = [sb(f"x{i}", [P, T, C]) for i in range(5)]
        wqkv_a, wout_a = sb("wqkv_a", [P, 3 * C]), sb("wout_a", [P, C])
        wqkv_b, wout_b = sb("wqkv_b", [P, 3 * C]), sb("wout_b", [P, C])
        w1, w2 = sb("w1", [P, FF]), sb("w2", [P, NF, C])
        BIAS = [("a_qkv", a_bqkv, 3 * C), ("a_out", a_bout, C), ("f1", f_b1, FF), ("f2", f_b2, C),
                ("b_qkv", b_bqkv, 3 * C), ("b_out", b_bout, C)]
        nb = sum(n for _, _, n in BIAS)
        bias32 = sb("bias32", [P, nb])
        bias_rest = sb("bias_rest", [P, nb])
        bias_part = sb("bias_part", [P, 3, nb], BF16)
        bias = sb("bias", [P, nb], BF16)
        at, bias_at = 0, {}
        for name, _, n in BIAS:
            bias_at[name] = slice(at, at + n)
            at += n
        ones = sb("ones", [P, P], BF16)
        wait_carrier = sb("wait_carrier", [P, 1])
        minus_one, minus_half = sb("minus_one", [P, 1]), sb("minus_half", [P, 1])
        ident = sb("ident", [P, P])
        head_mask = sb("head_mask", [P, HEADS, HD])
        quad_mask = sb("quad_mask", [P, HQ, HD])

        LN = ("a", "f1", "b", "f2")
        sums = {k: sb(f"sums_{k}", [P, 2, 6]) for k in LN}
        mv = {k: sb(f"mv_{k}", [P, 2, 2]) for k in LN}
        spread = {k: sb(f"spread_{k}", [P, 2, 1]) for k in LN}
        minus = {k: sb(f"minus_{k}", [P, 2, 1]) for k in LN}
        rstd = {k: sb(f"rstd_{k}", [P, 2, 1]) for k in LN}
        shift = {k: sb(f"shift_{k}", [P, 2, 1]) for k in LN}
        xn = {k: sb(f"xn_{k}", [P, 2, C]) for k in LN}
        xnT = {k: sb(f"xnT_{k}", [P, 2, P]) for k in LN}

        q_a = sb("q_a", [P, 2, C])
        k_a = sb("k_a", [P, 2, NW, C])
        vT_a = sb("vT_a", [P, 2, P])
        gram = sb("gram", [P, 2, NW, HQ, HD])
        gram_own = sb("gram_own", [P, 2, NW, HQ, HD])
        logit = sb("logit", [P, NW, HD])
        logit_max = sb("logit_max", [P, NW])
        logit_low = sb("logit_low", [P, 2, NW, HD])
        e_a = sb("e_a", [P, 2, NW, HD])
        e_sum_a = sb("e_sum_a", [P, NW])
        e_inv_a = sb("e_inv_a", [P, 2, NW])
        e_diag = sb("e_diag", [P, 2, NW, HEADS, HD])
        eT = sb("eT", [P, 2, NW, P])
        o_a = sb("o_a", [P, 2, NW * GROUPS, HD])
        o_wide = sb("o_wide", [P, 2, NW * GROUPS, HQ, HD])
        o_turned = sb("o_turned", [P, 2, HQ, NW * GROUPS, HD])

        hT = {k: sb(f"hT_{k}", [P, 2, NF, P]) for k in ("f1", "f2")}

        qkv_b = sb("qkv_b", [P, 2, HEADS, 3, HD])
        HH = HEADS // 2
        qk = sb("qk", [P, 2, HH, HEADS, HD])
        pv = sb("pv", [P, 2, HH, HD, HEADS])
        s_b = sb("s_b", [P, HEADS, HEADS])
        s_max = sb("s_max", [P, HEADS])
        s_low = sb("s_low", [P, 2, HEADS, HEADS])
        p_b = sb("p_b", [P, 2, HEADS, HEADS])
        p_sum = sb("p_sum", [P, HEADS])
        p_inv = sb("p_inv", [P, HEADS])
        c_raw = sb("c_raw", [P, HEADS, HD])
        c_b = sb("c_b", [P, 2, HEADS, HD])
        cT_b = sb("cT_b", [P, 2, P])

        def bank(name):
            return ctx.enter_context(nc.psum_tensor(name, [P, 512], F32))

        ps_in, ps_gram, ps_eT, ps_out = bank("ps_in"), bank("ps_gram"), bank("ps_eT"), bank("ps_out")
        ps_f = {k: bank(f"ps_{k}") for k in ("f1", "f2")}
        ps_b = [bank("ps_b0"), bank("ps_b1")]

        n_early = 2
        xw_in = [sem("xw_first_in"), sem("xw_rest_in")]
        windows_loads = [16 * NW, 16 * NW * B]
        x_in = sem("x_in")
        w_in = {k: sem(f"w_{k}_in") for k in ("a_qkv", "a_out", "f", "b")}
        bias_in = sem("bias_in")
        bias_steps, bias_ready = sem("bias_steps"), sem("bias_ready")
        const_steps, scalars_ready = sem("const_steps"), sem("scalars_ready")
        ident_ready, masks_ready = sem("ident_ready"), sem("masks_ready")
        zeros_ready, ones_ready = sem("zeros_ready"), sem("ones_ready")
        ln_sums = {k: sem(f"ln_sums_{k}") for k in LN}
        ln_mv = {k: sem(f"ln_mv_{k}") for k in LN}
        ln_spread = {k: sem(f"ln_spread_{k}") for k in LN}
        ln_minus = {k: sem(f"ln_minus_{k}") for k in LN}
        ln_rstd = {k: sem(f"ln_rstd_{k}") for k in LN}
        ln_ready = {k: sem(f"ln_ready_{k}") for k in LN}
        xn_ready = {k: sem(f"xn_ready_{k}") for k in LN}
        xnT_psum = {k: sem(f"xnT_psum_{k}") for k in LN}
        xnT_ready = {k: sem(f"xnT_ready_{k}") for k in LN}
        x_ready = [x_in] + [sem(f"x{i}_ready") for i in range(1, 5)]
        qkv_psum_a, qk_ready_a, v_ready_a = sem("qkv_psum_a"), sem("qk_ready_a"), sem("v_ready_a")
        gram_psum, gram_ready, gram_own_ready = sem("gram_psum"), sem("gram_ready"), sem("gram_own_ready")
        logit_ready, logit_max_ready, logit_low_ready = (
            sem("logit_ready"), sem("logit_max_ready"), sem("logit_low_ready"))
        e_ready_a, e_sum_ready_a, e_inv_ready_a = sem("e_ready_a"), sem("e_sum_ready_a"), sem("e_inv_ready_a")
        e_diag_ready, eT_psum, eT_ready = sem("e_diag_ready"), sem("eT_psum"), sem("eT_ready")
        o_psum, o_ready, o_wide_ready, o_turned_ready = (
            sem("o_psum"), sem("o_ready"), sem("o_wide_ready"), sem("o_turned_ready"))
        y_psum = {k: sem(f"y_psum_{k}") for k in LN}
        h_psum = {k: sem(f"h_psum_{k}") for k in ("f1", "f2")}
        h_ready = {k: sem(f"h_ready_{k}") for k in ("f1", "f2")}
        qkv_psum_b, qkv_ready_b = sem("qkv_psum_b"), sem("qkv_ready_b")
        qk_ready_b = [sem("qk_ready_b0"), sem("qk_ready_b1")]
        s_ready = [sem("s_ready0"), sem("s_ready1")]
        s_max_ready, s_low_ready, p_ready = sem("s_max_ready"), sem("s_low_ready"), sem("p_ready")
        p_sum_ready, p_inv_ready = sem("p_sum_ready"), sem("p_inv_ready")
        pv_ready = [sem("pv_ready0"), sem("pv_ready1")]
        c_raw_ready = [sem("c_raw_ready0"), sem("c_raw_ready1")]
        c_ready, cT_psum, cT_ready = sem("c_ready"), sem("cT_psum"), sem("cT_ready")
        out_stored = sem("out_stored")

        LN_IN = {"a": None, "f1": 1, "b": 2, "f2": 3}
        FFN = {"f1": (1, 2), "f2": (3, 4)}

        x_rows = x.rearrange("b (i m j) c -> j m (b i) c", j=GROUPS, m=P // GROUPS)
        out_rows = out.rearrange("b (i m j) c -> (b i) j m c", j=GROUPS, m=P // GROUPS)

        block = ctx.enter_context(nc.Block())

        @block.sync
        def _(sp):
            def load_windows(first, last, done):
                for b in range(B):
                    lo, hi = max(first, b * TPB), min(last, (b + 1) * TPB)
                    if lo >= hi:
                        continue
                    for n in range(NW):
                        at = (lo - b * TPB) * HOP_T + n * HOP
                        src = x[b, at:at + WIN, :]
                        src = bass.AP(src.tensor, src.offset, [[C, WIN], [HOP_T * C, hi - lo], [1, C]])
                        sp.dma_start(xw[WIN * n:WIN * (n + 1), lo:hi, :], src).then_inc(done, 16)

            load_windows(0, n_early, xw_in[0])
            sp.dma_start(wqkv_a[:, :], a_wqkv).then_inc(w_in["a_qkv"], 16)
            load_windows(n_early, T, xw_in[1])
            sp.dma_start(wout_a[:, :], a_wout).then_inc(w_in["a_out"], 16)
            for j in range(GROUPS):
                sp.dma_start(xs[0][P // GROUPS * j:P // GROUPS * (j + 1), :, :], x_rows[j]).then_inc(x_in, 16)
            sp.dma_start(w1[:, :], f_w1).then_inc(w_in["f"], 16)
            sp.dma_start(w2[:, :, :], f_w2.rearrange("(k p) c -> p k c", p=P)).then_inc(w_in["f"], 16)
            sp.dma_start(wqkv_b[:, :], b_wqkv).then_inc(w_in["b"], 16)
            sp.dma_start(wout_b[:, :], b_wout).then_inc(w_in["b"], 16)

            def store(t):
                wait(sp, x_ready[4], t.n + 1)
                sp.dma_start(out_rows[t.n], xs[4][:, t.n, :]).then_inc(out_stored, 16)

            with sp.Fori(0, T) as t:
                store(Tile(t, None))
            sp.wait_ge(out_stored, 16 * T)

        @block.gpsimd
        def _(pool):
            nc.gpsimd.memset(ident[:, :], 0.0).then_inc(const_steps, 1)
            nc.gpsimd.memset(head_mask[:, :, :], 1.0).then_inc(const_steps, 1)
            nc.gpsimd.memset(k_a[:, :, :, :], 0.0).then_inc(zeros_ready, 1)
            nc.gpsimd.memset(bias[:, :], 0.0).then_inc(zeros_ready, 1)
            nc.gpsimd.memset(ones[:, :], 1.0).then_inc(ones_ready, 1)
            nc.gpsimd.memset(minus_one[:, :], -1.0).then_inc(scalars_ready, 1)
            nc.gpsimd.memset(minus_half[:, :], -0.5).then_inc(scalars_ready, 1)
            pool.wait_ge(const_steps, 2)
            nc.gpsimd.affine_select(out=ident[:, :], in_=ident[:, :], compare_op=ALU.not_equal, fill=1.0,
                                    base=0, pattern=[[-1, P]], channel_multiplier=1).then_inc(ident_ready, 1)
            nc.gpsimd.affine_select(out=head_mask[:, :, :], in_=head_mask[:, :, :], compare_op=ALU.is_ge,
                                    fill=0.0, base=0, pattern=[[-HD, HEADS], [0, HD]],
                                    channel_multiplier=1).then_inc(const_steps, 1)
            pool.wait_ge(const_steps, 3)
            nc.gpsimd.affine_select(out=head_mask[:, :, :], in_=head_mask[:, :, :], compare_op=ALU.is_ge,
                                    fill=0.0, base=HD - 1, pattern=[[HD, HEADS], [0, HD]],
                                    channel_multiplier=-1).then_inc(const_steps, 1)
            pool.wait_ge(const_steps, 4)
            pool.wait_ge(scalars_ready, 2)
            pool.wait_ge(masks_ready, 1)

            def scales(k, t):
                h = t.half
                wait(pool, ln_mv[k], t.n + 1)
                wait(pool, xn_ready[k], t.n - 1)
                nc.gpsimd.tensor_tensor(minus[k][:, h, :], mv[k][:, h, 0:1], minus_one[:, :], ALU.mult
                                        ).then_inc(ln_minus[k], 1)
                wait(pool, ln_spread[k], t.n + 1)
                nc.gpsimd.tensor_tensor(rstd[k][:, h, :], spread[k][:, h, :], minus_half[:, :], ALU.pow
                                        ).then_inc(ln_rstd[k], 1)
                wait(pool, ln_minus[k], t.n + 1)
                wait(pool, ln_rstd[k], t.n + 1)
                nc.gpsimd.tensor_tensor(shift[k][:, h, :], minus[k][:, h, :], rstd[k][:, h, :], ALU.mult
                                        ).then_inc(ln_ready[k], 1)

            def front(k):
                return lambda t: scales(k, t)

            def a_softmax(t):
                wait(pool, gram_ready, t.n + 1)
                wait(pool, logit_ready, t.n - 1)
                nc.gpsimd.tensor_tensor(gram_own[:, t.half], gram[:, t.half],
                                        quad_mask[:, :, :].unsqueeze(1).broadcast_to([P, NW, HQ, HD]),
                                        ALU.mult).then_inc(gram_own_ready, 1)
                wait(pool, e_ready_a, t.n + 1)
                wait(pool, eT_psum, t.n - 1)
                nc.gpsimd.tensor_tensor(
                    e_diag[:, t.half],
                    e_a[:, t.half].unsqueeze(2).broadcast_to([P, NW, HEADS, HD]),
                    head_mask[:, :, :].unsqueeze(1).broadcast_to([P, NW, HEADS, HD]),
                    ALU.mult).then_inc(e_diag_ready, 1)

            def a_context(t):
                wait(pool, o_ready, t.n + 1)
                wait(pool, o_turned_ready, t.n - 1)
                nc.gpsimd.tensor_tensor(
                    o_wide[:, t.half],
                    o_a[:, t.half].unsqueeze(2).broadcast_to([P, NW * GROUPS, HQ, HD]),
                    quad_mask[:, :, :].unsqueeze(1).broadcast_to([P, NW * GROUPS, HQ, HD]),
                    ALU.mult).then_inc(o_wide_ready, 1)

            walk(pool, T, {"a_front": front("a"), "f1_up": front("f1"), "b_front": front("b"),
                           "f2_up": front("f2"), "a_softmax": a_softmax, "a_context": a_context})

        @block.scalar
        def _(act):
            at = 0
            for name, b, n in BIAS:
                act.dma_start(bias32[:, at:at + n], b.rearrange("(a n) -> a n", a=1).broadcast_to([P, n])
                              ).then_inc(bias_in, 16)
                at += n

            act.wait_ge(const_steps, 4)
            for g in range(P // QUAD):
                rows = slice(QUAD * g, QUAD * (g + 1))
                last = nc.scalar.activation(quad_mask[rows, :, :], head_mask[rows, HQ * g:HQ * (g + 1), :],
                                            ACT.Copy)
            last.then_inc(masks_ready, 1)

            def normalise(k, t):
                src = xw if k == "a" else xs[LN_IN[k]]
                wait(act, ln_ready[k], t.n + 1)
                wait(act, xnT_psum[k], t.n - 1)
                nc.scalar.activation(xn[k][:, t.half, :], src[:, t.n, :], ACT.Identity,
                                     bias=shift[k][:, t.half, :], scale=rstd[k][:, t.half, :]
                                     ).then_inc(xn_ready[k], 1)

            def copy_xnT(k, t, psum, reader):
                wait(act, xnT_psum[k], t.n + 1)
                wait(act, reader, t.n - 1)
                nc.scalar.activation(xnT[k][:, t.half, :], psum, ACT.Copy).then_inc(xnT_ready[k], 1)

            def a_front(t):
                normalise("a", t)
                copy_xnT("a", t, ps_in[:, 3 * C:4 * C], qkv_psum_a)
                wait(act, qkv_psum_a, t.n + 1)
                wait(act, gram_psum, t.n - 1)
                if isinstance(t.n, int) and t.n == 0:
                    act.wait_ge(zeros_ready, 2)
                nc.scalar.activation(q_a[:, t.half, :], ps_in[:, 0:C], ACT.Copy)
                for n in range(NW):
                    rows = slice(WIN * n, WIN * (n + 1))
                    last = nc.scalar.activation(k_a[rows, t.half, n, :], ps_in[rows, C:2 * C], ACT.Copy)
                last.then_inc(qk_ready_a, 1)
                wait(act, o_psum, t.n - 1)
                nc.scalar.activation(vT_a[:, t.half, :], ps_in[:, 2 * C:3 * C], ACT.Copy
                                     ).then_inc(v_ready_a, 1)
                wait(act, gram_psum, t.n + 1)
                wait(act, gram_own_ready, t.n - 1)
                pg = ps_gram[:, :].rearrange("p (n c) -> p n c", n=NW)
                for g in range(P // QUAD):
                    rows = slice(QUAD * g, QUAD * (g + 1))
                    last = nc.scalar.activation(gram[rows, t.half].rearrange("p n h e -> p n (h e)"),
                                                pg[rows, :, rows], ACT.Copy)
                last.then_inc(gram_ready, 1)

            def a_softmax(t):
                wait(act, logit_low_ready, t.n + 1)
                wait(act, e_inv_ready_a, t.n - 1)
                wait(act, e_diag_ready, t.n - 1)
                nc.scalar.activation(e_a[:, t.half], logit_low[:, t.half], ACT.Exp, scale=SCALE
                                     ).then_inc(e_ready_a, 1)
                wait(act, eT_psum, t.n + 1)
                wait(act, o_psum, t.n - 1)
                nc.scalar.activation(eT[:, t.half].rearrange("p n c -> p (n c)"), ps_eT[:, :], ACT.Copy
                                     ).then_inc(eT_ready, 1)

            def up(k):
                def run(t):
                    normalise(k, t)
                    copy_xnT(k, t, ps_f[k][:, 0:P], h_psum[k])
                    wait(act, h_psum[k], t.n + 1)
                    wait(act, y_psum[k], t.n - 1)
                    nc.scalar.activation(hT[k][:, t.half].rearrange("p k c -> p (k c)"), ps_f[k][:, :],
                                         ACT.Gelu).then_inc(h_ready[k], 1)
                return run

            def b_front(t):
                ps = ps_b[t.half]
                normalise("b", t)
                copy_xnT("b", t, ps[:, 3 * C:4 * C], qkv_psum_b)
                wait(act, qkv_psum_b, t.n + 1)
                wait(act, c_ready, t.n - 1)
                nc.scalar.activation(qkv_b[:, t.half].rearrange("p h s d -> p (h s d)"), ps[:, 0:3 * C],
                                     ACT.Copy).then_inc(qkv_ready_b, 1)

            def b_softmax(t):
                wait(act, s_low_ready, t.n + 1)
                wait(act, c_raw_ready[1], t.n - 1)
                nc.scalar.activation(p_b[:, t.half], s_low[:, t.half], ACT.Exp, scale=SCALE
                                     ).then_inc(p_ready, 1)

            def b_project(t):
                wait(act, cT_psum, t.n + 1)
                wait(act, y_psum["b"], t.n - 1)
                nc.scalar.activation(cT_b[:, t.half, :], ps_b[t.half][:, 3 * C:4 * C], ACT.Copy
                                     ).then_inc(cT_ready, 1)

            walk(act, T, {"a_front": a_front, "a_softmax": a_softmax, "f1_up": up("f1"), "f2_up": up("f2"),
                          "b_front": b_front, "b_softmax": b_softmax, "b_project": b_project})

        @block.vector
        def _(dve):
            dve.wait_ge(bias_in, 16 * len(BIAS))
            dve.wait_ge(zeros_ready, 2)
            steps = 0
            src = bias32
            for k in range(3):
                nc.vector.tensor_copy(bias_part[:, k, :], src[:, :]).then_inc(bias_steps, 1)
                steps += 1
                dve.wait_ge(bias_steps, steps)
                row = slice(QUAD * k, QUAD * k + 1)
                last = nc.vector.tensor_copy(bias[row, :], bias_part[row, k, :])
                if k < 2:
                    nc.vector.tensor_tensor(bias_rest[:, :], src[:, :], bias_part[:, k, :],
                                            ALU.subtract).then_inc(bias_steps, 1)
                    steps += 1
                    dve.wait_ge(bias_steps, steps)
                    src = bias_rest
            last.then_inc(bias_ready, 1)

            def alone(eng):
                eng.wait_ge(zeros_ready, 1)

            def statistics(k, t):
                src = xw if k == "a" else xs[LN_IN[k]]
                if k != "a":
                    alone(dve)
                    wait(dve, x_ready[LN_IN[k]], t.n + 1)
                elif isinstance(t.n, int) and t.n in (0, n_early):
                    i = int(t.n > 0)
                    dve.wait_ge(xw_in[i], windows_loads[i])
                h = t.half
                nc.vector.bn_stats(sums[k][:, h, :], src[:, t.n, :]).then_inc(ln_sums[k], 1)
                wait(dve, ln_sums[k], t.n + 1)
                nc.vector.memset(wait_carrier[:, :], 0.0)
                nc.vector.bn_aggr(mv[k][:, h, :], sums[k][:, h, :]).then_inc(ln_mv[k], 1)
                wait(dve, ln_mv[k], t.n + 1)
                wait(dve, ln_ready[k], t.n - 1)
                nc.vector.tensor_scalar_add(spread[k][:, h, :], mv[k][:, h, 1:2], EPS).then_inc(ln_spread[k], 1)

            def add_residual(k, t, src, dst, psum):
                wait(dve, y_psum[k], t.n + 1)
                if k == "a" and isinstance(t.n, int) and t.n == 0:
                    dve.wait_ge(x_in, 16 * GROUPS)
                nc.vector.tensor_tensor(xs[dst][:, t.n, :], psum, xs[src][:, t.n, :], ALU.add
                                        ).then_inc(x_ready[dst], 1)

            def a_front(t):
                statistics("a", t)

            def a_softmax(t):
                h = t.half
                wait(dve, gram_own_ready, t.n + 1)
                nc.vector.tensor_reduce(logit[:, :, :], gram_own[:, h].rearrange("p n h e -> p n e h"),
                                        AX_X, ALU.add).then_inc(logit_ready, 1)
                wait(dve, logit_ready, t.n + 1)
                nc.vector.tensor_reduce(logit_max[:, :], logit[:, :, :], AX_X, ALU.max
                                        ).then_inc(logit_max_ready, 1)
                wait(dve, logit_max_ready, t.n + 1)
                wait(dve, e_ready_a, t.n - 1)
                nc.vector.tensor_tensor(logit_low[:, h], logit[:, :, :],
                                        logit_max[:, :].unsqueeze(2).broadcast_to([P, NW, HD]),
                                        ALU.subtract).then_inc(logit_low_ready, 1)
                wait(dve, e_ready_a, t.n + 1)
                nc.vector.tensor_reduce(e_sum_a[:, :], e_a[:, h], AX_X, ALU.add).then_inc(e_sum_ready_a, 1)
                wait(dve, e_sum_ready_a, t.n + 1)
                nc.vector.reciprocal(e_inv_a[:, h, :], e_sum_a[:, :]).then_inc(e_inv_ready_a, 1)

            def a_context(t):
                wait(dve, o_psum, t.n + 1)
                wait(dve, e_inv_ready_a, t.n + 1)
                wait(dve, o_wide_ready, t.n - 1)
                nc.vector.tensor_tensor(
                    o_a[:, t.half].rearrange("p (j n) c -> p n j c", n=NW),
                    ps_out[:, 0:P].rearrange("p (n j c) -> p n j c", n=NW, j=GROUPS),
                    e_inv_a[:, t.half, :].unsqueeze(2).unsqueeze(3).broadcast_to([P, NW, GROUPS, HD]),
                    ALU.mult).then_inc(o_ready, 1)

            def a_project(t):
                wait(dve, o_wide_ready, t.n + 1)
                wait(dve, y_psum["a"], t.n - 1)
                nc.vector.transpose(o_turned[:, t.half].rearrange("p h m d -> p m h d"),
                                    o_wide[:, t.half]).then_inc(o_turned_ready, 1)
                add_residual("a", t, 0, 1, ps_out[:, C:2 * C])

            def up(k):
                return lambda t: statistics(k, t)

            def down(k):
                return lambda t: add_residual(k, t, *FFN[k], ps_f[k][:, 0:C])

            def b_scores(j):
                def run(t):
                    heads = slice(HH * j, HH * (j + 1))
                    q = qkv_b[:, t.half, heads, 0, :].unsqueeze(2).broadcast_to([P, HH, HEADS, HD])
                    k = ps_b[t.half][:, 0:3 * C].rearrange("p (h s d) -> p h s d", s=3, d=HD)[:, :, 1, :]
                    k = k.unsqueeze(1).broadcast_to([P, HH, HEADS, HD])
                    wait(dve, qkv_ready_b, t.n + 1)
                    nc.vector.tensor_tensor(qk[:, j], k, q, ALU.mult).then_inc(qk_ready_b[j], 1)
                    wait(dve, qk_ready_b[j], t.n + 1)
                    nc.vector.tensor_reduce(s_b[:, heads, :], qk[:, j], AX_X, ALU.add).then_inc(s_ready[j], 1)
                return run

            def b_softmax(t):
                h = t.half
                for j in range(2):
                    wait(dve, s_ready[j], t.n + 1)
                nc.vector.tensor_reduce(s_max[:, :], s_b[:, :, :], AX_X, ALU.max).then_inc(s_max_ready, 1)
                wait(dve, s_max_ready, t.n + 1)
                wait(dve, p_ready, t.n - 1)
                nc.vector.tensor_tensor(s_low[:, h], s_b[:, :, :],
                                        s_max[:, :].unsqueeze(2).broadcast_to([P, HEADS, HEADS]),
                                        ALU.subtract).then_inc(s_low_ready, 1)

            def b_context(j):
                def run(t):
                    h = t.half
                    heads = slice(HH * j, HH * (j + 1))
                    v = ps_b[h][:, 0:3 * C].rearrange("p (h s d) -> p d s h", s=3, d=HD)[:, :, 2, :]
                    v = v.unsqueeze(1).broadcast_to([P, HH, HD, HEADS])
                    p = p_b[:, h, heads, :].unsqueeze(2).broadcast_to([P, HH, HD, HEADS])
                    wait(dve, p_ready, t.n + 1)
                    nc.vector.tensor_tensor(pv[:, j], v, p, ALU.mult).then_inc(pv_ready[j], 1)
                    if j == 0:
                        nc.vector.tensor_reduce(p_sum[:, :], p_b[:, h], AX_X, ALU.add).then_inc(p_sum_ready, 1)
                    wait(dve, pv_ready[j], t.n + 1)
                    nc.vector.tensor_reduce(c_raw[:, heads, :], pv[:, j], AX_X, ALU.add
                                            ).then_inc(c_raw_ready[j], 1)
                    if j == 0:
                        wait(dve, p_sum_ready, t.n + 1)
                        nc.vector.reciprocal(p_inv[:, :], p_sum[:, :]).then_inc(p_inv_ready, 1)
                        return
                    wait(dve, p_inv_ready, t.n + 1)
                    for i in range(2):
                        wait(dve, c_raw_ready[i], t.n + 1)
                    wait(dve, cT_psum, t.n - 1)
                    nc.vector.tensor_tensor(c_b[:, h], c_raw[:, :, :],
                                            p_inv[:, :].unsqueeze(2).broadcast_to([P, HEADS, HD]),
                                            ALU.mult).then_inc(c_ready, 1)
                return run

            def b_residual(t):
                add_residual("b", t, 2, 3, ps_b[t.half][:, 0:C])

            def b_front(t):
                statistics("b", t)

            walk(dve, T, {"a_front": a_front, "a_softmax": a_softmax, "a_context": a_context,
                          "a_project": a_project, "f1_up": up("f1"), "f2_up": up("f2"),
                          "f1_down": down("f1"), "f2_down": down("f2"), "b_front": b_front,
                          "b_scores_0": b_scores(0), "b_scores_1": b_scores(1), "b_softmax": b_softmax,
                          "b_context_0": b_context(0), "b_context_1": b_context(1),
                          "b_residual": b_residual})

        @block.tensor
        def _(pe):
            pe.wait_ge(ident_ready, 1)
            pe.wait_ge(ones_ready, 1)

            def mm(psum, lhsT, rhs, start=False, stop=False):
                return nc.tensor.matmul(psum, lhsT, rhs, start=start, stop=stop)

            def turn(k, t, psum):
                wait(pe, xn_ready[k], t.n + 1)
                nc.tensor.transpose(psum, xn[k][:, t.half, :], ident[:, :]).then_inc(xnT_psum[k], 1)

            def first(t):
                return isinstance(t.n, int) and t.n == 0

            def a_front(t):
                wait(pe, v_ready_a, t.n)
                turn("a", t, ps_in[:, 3 * C:4 * C])
                wait(pe, xnT_ready["a"], t.n + 1)
                if first(t):
                    pe.wait_ge(w_in["a_qkv"], 16)
                    pe.wait_ge(bias_ready, 1)
                xT = xnT["a"][:, t.half, :]
                b = bias[:, bias_at["a_qkv"]]
                mm(ps_in[:, 0:2 * C], xT, wqkv_a[:, 0:2 * C], start=True)
                mm(ps_in[:, 0:2 * C], ones[:, :], b[:, 0:2 * C], stop=True)
                mm(ps_in[:, 2 * C:3 * C], wqkv_a[:, 2 * C:3 * C], xT, start=True)
                mm(ps_in[:, 2 * C:3 * C], b[:, 2 * C:3 * C], ones[:, :], stop=True).then_inc(qkv_psum_a, 1)
                wait(pe, qk_ready_a, t.n + 1)
                wait(pe, gram_ready, t.n)
                mm(ps_gram[:, :], q_a[:, t.half, :], k_a[:, t.half].rearrange("p n c -> p (n c)"),
                   start=True, stop=True).then_inc(gram_psum, 1)

            def a_softmax(t):
                wait(pe, e_diag_ready, t.n + 1)
                wait(pe, eT_ready, t.n)
                for n in range(NW):
                    last = nc.tensor.transpose(ps_eT[:, P * n:P * (n + 1)],
                                               e_diag[:, t.half, n].rearrange("p h e -> p (h e)"), ident[:, :])
                last.then_inc(eT_psum, 1)

            def a_context(t):
                wait(pe, eT_ready, t.n + 1)
                wait(pe, v_ready_a, t.n + 1)
                wait(pe, x_ready[1], t.n)
                for n in range(NW):
                    cols = slice(WIN * n, WIN * (n + 1))
                    last = mm(ps_out[:, cols], eT[:, t.half, n, :], vT_a[:, t.half, cols], start=True, stop=True)
                last.then_inc(o_psum, 1)

            def a_project(t):
                wait(pe, o_turned_ready, t.n + 1)
                wait(pe, o_ready, t.n + 1)
                if first(t):
                    pe.wait_ge(w_in["a_out"], 16)
                for i in range(HQ):
                    mm(ps_out[:, C:2 * C], o_turned[:, t.half, i].rearrange("p m d -> p (m d)"),
                       wout_a[:, :], start=i == 0)
                mm(ps_out[:, C:2 * C], ones[:, :], bias[:, bias_at["a_out"]], stop=True
                   ).then_inc(y_psum["a"], 1)

            def up(k):
                def run(t):
                    wait(pe, x_ready[FFN[k][1]], t.n)
                    turn(k, t, ps_f[k][:, 0:P])
                    if first(t):
                        pe.wait_ge(w_in["f"], 32)
                    wait(pe, xnT_ready[k], t.n + 1)
                    for i in range(NF):
                        cols = slice(P * i, P * (i + 1))
                        mm(ps_f[k][:, cols], w1[:, cols], xnT[k][:, t.half, :], start=True)
                        last = mm(ps_f[k][:, cols], bias[:, bias_at["f1"]][:, cols], ones[:, :], stop=True)
                    last.then_inc(h_psum[k], 1)
                return run

            def down(k):
                def run(t):
                    wait(pe, h_ready[k], t.n + 1)
                    for i in range(NF):
                        mm(ps_f[k][:, 0:C], hT[k][:, t.half, i, :], w2[:, i, :], start=i == 0)
                    mm(ps_f[k][:, 0:C], ones[:, :], bias[:, bias_at["f2"]], stop=True).then_inc(y_psum[k], 1)
                return run

            def b_front(t):
                ps = ps_b[t.half]
                wait(pe, x_ready[3], t.n - 1)
                turn("b", t, ps[:, 3 * C:4 * C])
                if first(t):
                    pe.wait_ge(w_in["b"], 32)
                wait(pe, xnT_ready["b"], t.n + 1)
                mm(ps[:, 0:3 * C], xnT["b"][:, t.half, :], wqkv_b[:, :], start=True)
                mm(ps[:, 0:3 * C], ones[:, :], bias[:, bias_at["b_qkv"]], stop=True).then_inc(qkv_psum_b, 1)

            def b_project(t):
                ps = ps_b[t.half]
                wait(pe, c_ready, t.n + 1)
                nc.tensor.transpose(ps[:, 3 * C:4 * C], c_b[:, t.half].rearrange("p h d -> p (h d)"),
                                    ident[:, :]).then_inc(cT_psum, 1)
                wait(pe, cT_ready, t.n + 1)
                mm(ps[:, 0:C], cT_b[:, t.half, :], wout_b[:, :], start=True)
                mm(ps[:, 0:C], ones[:, :], bias[:, bias_at["b_out"]], stop=True).then_inc(y_psum["b"], 1)

            walk(pe, T, {"a_front": a_front, "a_softmax": a_softmax, "a_context": a_context,
                         "a_project": a_project, "f1_up": up("f1"), "f2_up": up("f2"), "f1_down": down("f1"),
                         "f2_down": down("f2"), "b_front": b_front, "b_project": b_project})


_INS = ["L0_attn_a_x", "L0_attn_a_W_qkv", "L0_attn_a_b_qkv", "L0_attn_a_W_out", "L0_attn_a_b_out",
        "L0_attn_b_W_qkv", "L0_attn_b_b_qkv", "L0_attn_b_W_out", "L0_attn_b_b_out",
        "L0_ffn_w1", "L0_ffn_b1", "L0_ffn_w2", "L0_ffn_b2"]


def kernel(**inputs):
    import numpy as _np
    import concourse.bacc as _bacc
    from concourse import mybir as _mybir
    from concourse.bass_utils import run_bass_kernel_spmd as _run

    nc = _bacc.Bacc("TRN2", target_bir_lowering=False, num_devices=1)
    arrays, args = {}, []
    for name in _INS:
        a = _np.ascontiguousarray(inputs[name])
        arrays[f"in_{name}_dram"] = a
        args.append(nc.dram_tensor(f"in_{name}_dram", a.shape, _mybir.dt.from_np(a.dtype),
                                   kind="ExternalInput").ap())
    shape = inputs["L0_attn_a_x"].shape
    args.append(nc.dram_tensor("out_0_dram", shape, _mybir.dt.float32, kind="ExternalOutput").ap())
    hybrid_block(nc, *args)
    r = _run(nc, [arrays], core_ids=[0])
    return r.results[0]["out_0_dram"]
```

```python
from contextlib import ExitStack

import concourse.bass as bass
from concourse import mybir

P = 128
F32 = mybir.dt.float32
BF16 = mybir.dt.bfloat16
ALU = mybir.AluOpType
ACT = mybir.ActivationFunctionType
AX_X = mybir.AxisListType.X

HEADS = 16
HD = 8
WIN = 32
HOP = WIN // 2
EPS = 1e-5
SCALE = float(HD) ** -0.5
QUAD = 32
HQ = QUAD // HD
ROWS_PER_WIN = WIN
NW = P // ROWS_PER_WIN
GROUPS = WIN // HD

STEP = [("f1_norm", 3), ("a_norm", 0), ("b_qk_0", 5), ("a_gram", 1), ("b_qk_1", 5), ("b_s_0", 5),
        ("f1_turn", 3), ("b_qk_pool", 5), ("b_turn_out", 6), ("b_s_1", 5), ("b_project", 6),
        ("a_turn", 0), ("b_softmax", 5), ("a_logits", 1), ("f2_norm", 6), ("b_pv_0", 5),
        ("a_context", 2), ("f2_down", 7), ("f1_up", 3), ("f2_turn", 6), ("b_pv_pool", 5), ("b_norm", 4),
        ("b_pv_1", 5), ("a_exp", 1), ("b_sums", 5), ("a_qkv", 0), ("b_c_1", 5), ("f2_up", 6),
        ("b_turn", 4), ("a_turn_out", 2), ("a_sums", 1), ("b_c_0", 5), ("f1_down", 3), ("a_project", 2),
        ("a_spread", 1), ("b_qkv", 4), ("b_scale", 5)]
LAG = max(d for _, d in STEP)

MADE = [slice(0, 6), slice(6, 12)]
MADE_POOL = slice(12, HEADS)
SUMMED = [slice(0, 6), slice(6, HEADS)]


class Tile:

    def __init__(self, n, half):
        self.n, self.half = n, half


def wait(eng, sem, count):
    if isinstance(count, int) and count <= 0:
        return
    eng.wait_ge(sem, count)


def walk(eng, tiles, stages):
    def at(s):
        for name, lag in STEP:
            if name in stages and 0 <= s - lag < tiles:
                stages[name](Tile(s - lag, (s - lag) % 2))

    begin = LAG + 2
    for s in range(begin):
        at(s)
    with eng.Fori(0, (tiles - begin) // 2) as pair:
        for odd in range(2):
            for name, lag in STEP:
                if name in stages:
                    stages[name](Tile(pair * 2 + (begin + odd - lag), (begin + odd - lag) % 2))
    for s in range(begin + (tiles - begin) // 2 * 2, tiles + LAG):
        at(s)


def hybrid_block(nc, x, a_wqkv, a_bqkv, a_wout, a_bout, b_wqkv, b_bqkv, b_wout, b_bout,
                 f_w1, f_b1, f_w2, f_b2, out):
    B, L, C = x.shape
    FF = f_w1.shape[1]
    NF = FF // P
    TPB = L // P
    T = B * TPB
    assert C == P == HEADS * HD and NF * P == 512
    HOP_T = NW * HOP
    assert (L - P) // P * HOP_T + (NW - 1) * HOP + WIN <= L

    with ExitStack() as ctx:
        def sb(name, shape, dt=F32):
            return ctx.enter_context(nc.sbuf_tensor(name, shape, dt))

        def sem(name):
            return ctx.enter_context(nc.semaphore(name))

        xw = sb("xw", [P, T, C])
        xs = [sb(f"x{i}", [P, T, C]) for i in range(5)]
        wqkv_a, wout_a = sb("wqkv_a", [P, 3 * C]), sb("wout_a", [P, C])
        wqkv_b, wout_b = sb("wqkv_b", [P, 3 * C]), sb("wout_b", [P, C])
        w1, w2 = sb("w1", [P, FF]), sb("w2", [P, NF, C])
        BIAS = [("a_qkv", a_bqkv, 3 * C), ("a_out", a_bout, C), ("f1", f_b1, FF), ("f2", f_b2, C),
                ("b_qkv", b_bqkv, 3 * C), ("b_out", b_bout, C)]
        nb = sum(n for _, _, n in BIAS)
        bias32 = sb("bias32", [P, nb])
        bias_rest = sb("bias_rest", [P, nb])
        bias_part = sb("bias_part", [P, 3, nb], BF16)
        bias = sb("bias", [P, nb], BF16)
        at, bias_at = 0, {}
        for name, _, n in BIAS:
            bias_at[name] = slice(at, at + n)
            at += n
        ones = sb("ones", [P, P], BF16)
        wait_carrier = sb("wait_carrier", [P, 1])
        minus_one, minus_half = sb("minus_one", [P, 1]), sb("minus_half", [P, 1])
        ident = sb("ident", [P, P])
        head_mask = sb("head_mask", [P, HEADS, HD])
        quad_mask = sb("quad_mask", [P, HQ, HD])

        LN = ("a", "f1", "b", "f2")
        sums = {k: sb(f"sums_{k}", [P, 2, 6]) for k in LN}
        mv = {k: sb(f"mv_{k}", [P, 2, 2]) for k in LN}
        spread = {k: sb(f"spread_{k}", [P, 2, 1]) for k in LN}
        minus = {k: sb(f"minus_{k}", [P, 2, 1]) for k in LN}
        rstd = {k: sb(f"rstd_{k}", [P, 2, 1]) for k in LN}
        shift = {k: sb(f"shift_{k}", [P, 2, 1]) for k in LN}
        xn = {k: sb(f"xn_{k}", [P, 2, C]) for k in LN}
        xnT = {k: sb(f"xnT_{k}", [P, 2, P]) for k in LN}

        q_a = sb("q_a", [P, 2, C])
        k_a = sb("k_a", [P, 2, NW, C])
        vT_a = sb("vT_a", [P, 2, P])
        gram = sb("gram", [P, 2, NW, HQ, HD])
        gram_own = sb("gram_own", [P, 2, NW, HQ, HD])
        logit = sb("logit", [P, NW, HD])
        logit_max = sb("logit_max", [P, NW])
        logit_low = sb("logit_low", [P, 2, NW, HD])
        e_a = sb("e_a", [P, 2, NW, HD])
        e_sum_a = sb("e_sum_a", [P, NW])
        e_inv_a = sb("e_inv_a", [P, 2, NW])
        e_diag = sb("e_diag", [P, 2, NW, HEADS, HD])
        eT = sb("eT", [P, 2, NW, P])
        o_a = sb("o_a", [P, 2, NW * GROUPS, HD])
        o_wide = sb("o_wide", [P, 2, NW * GROUPS, HQ, HD])
        o_turned = sb("o_turned", [P, 2, HQ, NW * GROUPS, HD])

        hT = {k: sb(f"hT_{k}", [P, 2, NF, P]) for k in ("f1", "f2")}

        qkv_b = sb("qkv_b", [P, 2, HEADS, 3, HD])
        qk = sb("qk", [P, HEADS, HEADS, HD])
        pv = sb("pv", [P, HEADS, HD, HEADS])
        s_b = sb("s_b", [P, HEADS, HEADS])
        s_max = sb("s_max", [P, HEADS])
        s_low = sb("s_low", [P, 2, HEADS, HEADS])
        p_b = sb("p_b", [P, 2, HEADS, HEADS])
        p_sum = sb("p_sum", [P, HEADS])
        p_inv = sb("p_inv", [P, HEADS])
        c_raw = sb("c_raw", [P, HEADS, HD])
        c_b = sb("c_b", [P, 2, HEADS, HD])
        cT_b = sb("cT_b", [P, 2, P])

        def bank(name):
            return ctx.enter_context(nc.psum_tensor(name, [P, 512], F32))

        ps_in, ps_gram, ps_eT, ps_out = bank("ps_in"), bank("ps_gram"), bank("ps_eT"), bank("ps_out")
        ps_f = {k: bank(f"ps_{k}") for k in ("f1", "f2")}
        ps_b = [bank("ps_b0"), bank("ps_b1")]

        n_early = 2
        xw_in = [sem("xw_first_in"), sem("xw_rest_in")]
        windows_loads = [16 * NW, 16 * NW * B]
        x_in = sem("x_in")
        w_in = {k: sem(f"w_{k}_in") for k in ("a_qkv", "a_out", "f", "b")}
        bias_in = sem("bias_in")
        bias_steps, bias_ready = sem("bias_steps"), sem("bias_ready")
        const_steps, scalars_ready = sem("const_steps"), sem("scalars_ready")
        ident_ready, masks_ready = sem("ident_ready"), sem("masks_ready")
        zeros_ready, ones_ready = sem("zeros_ready"), sem("ones_ready")
        ln_sums = {k: sem(f"ln_sums_{k}") for k in LN}
        ln_mv = {k: sem(f"ln_mv_{k}") for k in LN}
        ln_spread = {k: sem(f"ln_spread_{k}") for k in LN}
        ln_minus = {k: sem(f"ln_minus_{k}") for k in LN}
        ln_rstd = {k: sem(f"ln_rstd_{k}") for k in LN}
        ln_ready = {k: sem(f"ln_ready_{k}") for k in LN}
        xn_ready = {k: sem(f"xn_ready_{k}") for k in LN}
        xnT_psum = {k: sem(f"xnT_psum_{k}") for k in LN}
        xnT_ready = {k: sem(f"xnT_ready_{k}") for k in LN}
        x_ready = [x_in] + [sem(f"x{i}_ready") for i in range(1, 5)]
        qkv_psum_a, qk_ready_a, v_ready_a = sem("qkv_psum_a"), sem("qk_ready_a"), sem("v_ready_a")
        gram_psum, gram_ready, gram_own_ready = sem("gram_psum"), sem("gram_ready"), sem("gram_own_ready")
        logit_ready, logit_max_ready, logit_low_ready = (
            sem("logit_ready"), sem("logit_max_ready"), sem("logit_low_ready"))
        e_ready_a, e_sum_ready_a, e_inv_ready_a = sem("e_ready_a"), sem("e_sum_ready_a"), sem("e_inv_ready_a")
        e_diag_ready, eT_psum, eT_ready = sem("e_diag_ready"), sem("eT_psum"), sem("eT_ready")
        o_psum, o_ready, o_wide_ready, o_turned_ready = (
            sem("o_psum"), sem("o_ready"), sem("o_wide_ready"), sem("o_turned_ready"))
        y_psum = {k: sem(f"y_psum_{k}") for k in LN}
        h_psum = {k: sem(f"h_psum_{k}") for k in ("f1", "f2")}
        h_ready = {k: sem(f"h_ready_{k}") for k in ("f1", "f2")}
        qkv_psum_b, qkv_ready_b = sem("qkv_psum_b"), sem("qkv_ready_b")
        qk_ready_b = [sem("qk_ready_b0"), sem("qk_ready_b1")]
        qk_ready_pool, pv_ready_pool = sem("qk_ready_pool"), sem("pv_ready_pool")
        s_ready = [sem("s_ready0"), sem("s_ready1")]
        s_max_ready, s_low_ready, p_ready = sem("s_max_ready"), sem("s_low_ready"), sem("p_ready")
        p_sum_ready, p_inv_ready = sem("p_sum_ready"), sem("p_inv_ready")
        pv_ready = [sem("pv_ready0"), sem("pv_ready1")]
        c_raw_ready = [sem("c_raw_ready0"), sem("c_raw_ready1")]
        c_ready, cT_psum, cT_ready = sem("c_ready"), sem("cT_psum"), sem("cT_ready")
        out_stored = sem("out_stored")

        LN_IN = {"a": None, "f1": 1, "b": 2, "f2": 3}
        FFN = {"f1": (1, 2), "f2": (3, 4)}

        x_rows = x.rearrange("b (i m j) c -> j m (b i) c", j=GROUPS, m=P // GROUPS)
        out_rows = out.rearrange("b (i m j) c -> (b i) j m c", j=GROUPS, m=P // GROUPS)

        def q_times_k(t, k, heads):
            shape = [P, heads.stop - heads.start, HEADS, HD]
            return (k.unsqueeze(1).broadcast_to(shape),
                    qkv_b[:, t.half, heads, 0, :].unsqueeze(2).broadcast_to(shape))

        def v_times_p(t, v, heads):
            shape = [P, heads.stop - heads.start, HD, HEADS]
            return (v.unsqueeze(1).broadcast_to(shape),
                    p_b[:, t.half, heads, :].unsqueeze(2).broadcast_to(shape))

        block = ctx.enter_context(nc.Block())

        @block.sync
        def _(sp):
            def load_windows(first, last, done):
                for b in range(B):
                    lo, hi = max(first, b * TPB), min(last, (b + 1) * TPB)
                    if lo >= hi:
                        continue
                    for n in range(NW):
                        at = (lo - b * TPB) * HOP_T + n * HOP
                        src = x[b, at:at + WIN, :]
                        src = bass.AP(src.tensor, src.offset, [[C, WIN], [HOP_T * C, hi - lo], [1, C]])
                        sp.dma_start(xw[WIN * n:WIN * (n + 1), lo:hi, :], src).then_inc(done, 16)

            load_windows(0, n_early, xw_in[0])
            sp.dma_start(wqkv_a[:, :], a_wqkv).then_inc(w_in["a_qkv"], 16)
            load_windows(n_early, T, xw_in[1])
            sp.dma_start(wout_a[:, :], a_wout).then_inc(w_in["a_out"], 16)
            for j in range(GROUPS):
                sp.dma_start(xs[0][P // GROUPS * j:P // GROUPS * (j + 1), :, :], x_rows[j]).then_inc(x_in, 16)
            sp.dma_start(w1[:, :], f_w1).then_inc(w_in["f"], 16)
            sp.dma_start(w2[:, :, :], f_w2.rearrange("(k p) c -> p k c", p=P)).then_inc(w_in["f"], 16)
            sp.dma_start(wqkv_b[:, :], b_wqkv).then_inc(w_in["b"], 16)
            sp.dma_start(wout_b[:, :], b_wout).then_inc(w_in["b"], 16)

            def store(t):
                wait(sp, x_ready[4], t.n + 1)
                sp.dma_start(out_rows[t.n], xs[4][:, t.n, :]).then_inc(out_stored, 16)

            with sp.Fori(0, T) as t:
                store(Tile(t, None))
            sp.wait_ge(out_stored, 16 * T)

        @block.gpsimd
        def _(pool):
            nc.gpsimd.memset(ident[:, :], 0.0).then_inc(const_steps, 1)
            nc.gpsimd.memset(head_mask[:, :, :], 1.0).then_inc(const_steps, 1)
            nc.gpsimd.memset(k_a[:, :, :, :], 0.0).then_inc(zeros_ready, 1)
            nc.gpsimd.memset(bias[:, :], 0.0).then_inc(zeros_ready, 1)
            nc.gpsimd.memset(ones[:, :], 1.0).then_inc(ones_ready, 1)
            nc.gpsimd.memset(minus_one[:, :], -1.0).then_inc(scalars_ready, 1)
            nc.gpsimd.memset(minus_half[:, :], -0.5).then_inc(scalars_ready, 1)
            pool.wait_ge(const_steps, 2)
            nc.gpsimd.affine_select(out=ident[:, :], in_=ident[:, :], compare_op=ALU.not_equal, fill=1.0,
                                    base=0, pattern=[[-1, P]], channel_multiplier=1).then_inc(ident_ready, 1)
            nc.gpsimd.affine_select(out=head_mask[:, :, :], in_=head_mask[:, :, :], compare_op=ALU.is_ge,
                                    fill=0.0, base=0, pattern=[[-HD, HEADS], [0, HD]],
                                    channel_multiplier=1).then_inc(const_steps, 1)
            pool.wait_ge(const_steps, 3)
            nc.gpsimd.affine_select(out=head_mask[:, :, :], in_=head_mask[:, :, :], compare_op=ALU.is_ge,
                                    fill=0.0, base=HD - 1, pattern=[[HD, HEADS], [0, HD]],
                                    channel_multiplier=-1).then_inc(const_steps, 1)
            pool.wait_ge(const_steps, 4)
            pool.wait_ge(scalars_ready, 2)
            pool.wait_ge(masks_ready, 1)

            def scales(k, t):
                h = t.half
                wait(pool, ln_mv[k], t.n + 1)
                wait(pool, xn_ready[k], t.n - 1)
                nc.gpsimd.tensor_tensor(minus[k][:, h, :], mv[k][:, h, 0:1], minus_one[:, :], ALU.mult
                                        ).then_inc(ln_minus[k], 1)
                wait(pool, ln_spread[k], t.n + 1)
                nc.gpsimd.tensor_tensor(rstd[k][:, h, :], spread[k][:, h, :], minus_half[:, :], ALU.pow
                                        ).then_inc(ln_rstd[k], 1)
                wait(pool, ln_minus[k], t.n + 1)
                wait(pool, ln_rstd[k], t.n + 1)
                nc.gpsimd.tensor_tensor(shift[k][:, h, :], minus[k][:, h, :], rstd[k][:, h, :], ALU.mult
                                        ).then_inc(ln_ready[k], 1)

            def norm(k):
                return lambda t: scales(k, t)

            def a_logits(t):
                wait(pool, gram_ready, t.n + 1)
                wait(pool, logit_ready, t.n - 1)
                nc.gpsimd.tensor_tensor(gram_own[:, t.half], gram[:, t.half],
                                        quad_mask[:, :, :].unsqueeze(1).broadcast_to([P, NW, HQ, HD]),
                                        ALU.mult).then_inc(gram_own_ready, 1)

            def a_spread(t):
                wait(pool, e_ready_a, t.n + 1)
                wait(pool, eT_psum, t.n - 1)
                nc.gpsimd.tensor_tensor(
                    e_diag[:, t.half],
                    e_a[:, t.half].unsqueeze(2).broadcast_to([P, NW, HEADS, HD]),
                    head_mask[:, :, :].unsqueeze(1).broadcast_to([P, NW, HEADS, HD]),
                    ALU.mult).then_inc(e_diag_ready, 1)

            def a_turn_out(t):
                wait(pool, o_ready, t.n + 1)
                wait(pool, o_turned_ready, t.n - 1)
                nc.gpsimd.tensor_tensor(
                    o_wide[:, t.half],
                    o_a[:, t.half].unsqueeze(2).broadcast_to([P, NW * GROUPS, HQ, HD]),
                    quad_mask[:, :, :].unsqueeze(1).broadcast_to([P, NW * GROUPS, HQ, HD]),
                    ALU.mult).then_inc(o_wide_ready, 1)

            def b_qk_pool(t):
                wait(pool, qkv_ready_b, t.n + 1)
                wait(pool, s_ready[1], t.n)
                nc.gpsimd.tensor_tensor(qk[:, MADE_POOL],
                                        *q_times_k(t, qkv_b[:, t.half, :, 1, :], MADE_POOL), ALU.mult
                                        ).then_inc(qk_ready_pool, 1)

            def b_pv_pool(t):
                wait(pool, p_ready, t.n + 1)
                wait(pool, c_raw_ready[1], t.n)
                nc.gpsimd.tensor_tensor(
                    pv[:, MADE_POOL],
                    *v_times_p(t, qkv_b[:, t.half, :, 2, :].rearrange("p h d -> p d h"), MADE_POOL),
                    ALU.mult).then_inc(pv_ready_pool, 1)

            walk(pool, T, {"b_qk_pool": b_qk_pool, "b_pv_pool": b_pv_pool, "a_norm": norm("a"), "f1_norm": norm("f1"), "b_norm": norm("b"),
                           "f2_norm": norm("f2"), "a_logits": a_logits, "a_spread": a_spread,
                           "a_turn_out": a_turn_out})

        @block.scalar
        def _(act):
            at = 0
            for name, b, n in BIAS:
                act.dma_start(bias32[:, at:at + n], b.rearrange("(a n) -> a n", a=1).broadcast_to([P, n])
                              ).then_inc(bias_in, 16)
                at += n

            act.wait_ge(const_steps, 4)
            for g in range(P // QUAD):
                rows = slice(QUAD * g, QUAD * (g + 1))
                last = nc.scalar.activation(quad_mask[rows, :, :], head_mask[rows, HQ * g:HQ * (g + 1), :],
                                            ACT.Copy)
            last.then_inc(masks_ready, 1)

            def normalise(k, t):
                src = xw if k == "a" else xs[LN_IN[k]]
                wait(act, ln_ready[k], t.n + 1)
                wait(act, xnT_psum[k], t.n - 1)
                nc.scalar.activation(xn[k][:, t.half, :], src[:, t.n, :], ACT.Identity,
                                     bias=shift[k][:, t.half, :], scale=rstd[k][:, t.half, :]
                                     ).then_inc(xn_ready[k], 1)

            def copy_xnT(k, t, psum, reader):
                wait(act, xnT_psum[k], t.n + 1)
                wait(act, reader, t.n - 1)
                nc.scalar.activation(xnT[k][:, t.half, :], psum, ACT.Copy).then_inc(xnT_ready[k], 1)

            def a_turn(t):
                copy_xnT("a", t, ps_in[:, 3 * C:4 * C], qkv_psum_a)

            def a_qkv(t):
                wait(act, qkv_psum_a, t.n + 1)
                wait(act, gram_psum, t.n - 1)
                if isinstance(t.n, int) and t.n == 0:
                    act.wait_ge(zeros_ready, 2)
                nc.scalar.activation(q_a[:, t.half, :], ps_in[:, 0:C], ACT.Copy)
                for n in range(NW):
                    rows = slice(WIN * n, WIN * (n + 1))
                    last = nc.scalar.activation(k_a[rows, t.half, n, :], ps_in[rows, C:2 * C], ACT.Copy)
                last.then_inc(qk_ready_a, 1)
                wait(act, o_psum, t.n - 1)
                nc.scalar.activation(vT_a[:, t.half, :], ps_in[:, 2 * C:3 * C], ACT.Copy
                                     ).then_inc(v_ready_a, 1)

            def a_gram(t):
                wait(act, gram_psum, t.n + 1)
                wait(act, gram_own_ready, t.n - 1)
                pg = ps_gram[:, :].rearrange("p (n c) -> p n c", n=NW)
                for g in range(P // QUAD):
                    rows = slice(QUAD * g, QUAD * (g + 1))
                    last = nc.scalar.activation(gram[rows, t.half].rearrange("p n h e -> p n (h e)"),
                                                pg[rows, :, rows], ACT.Copy)
                last.then_inc(gram_ready, 1)

            def a_exp(t):
                wait(act, logit_low_ready, t.n + 1)
                wait(act, e_inv_ready_a, t.n - 1)
                wait(act, e_diag_ready, t.n - 1)
                nc.scalar.activation(e_a[:, t.half], logit_low[:, t.half], ACT.Exp, scale=SCALE
                                     ).then_inc(e_ready_a, 1)

            def a_spread(t):
                wait(act, eT_psum, t.n + 1)
                wait(act, o_psum, t.n - 1)
                nc.scalar.activation(eT[:, t.half].rearrange("p n c -> p (n c)"), ps_eT[:, :], ACT.Copy
                                     ).then_inc(eT_ready, 1)

            def norm(k):
                return lambda t: normalise(k, t)

            def turn(k):
                return lambda t: copy_xnT(k, t, ps_f[k][:, 0:P], h_psum[k])

            def up(k):
                def run(t):
                    wait(act, h_psum[k], t.n + 1)
                    wait(act, y_psum[k], t.n - 1)
                    nc.scalar.activation(hT[k][:, t.half].rearrange("p k c -> p (k c)"), ps_f[k][:, :],
                                         ACT.Gelu).then_inc(h_ready[k], 1)
                return run

            def b_turn(t):
                copy_xnT("b", t, ps_b[t.half][:, 3 * C:4 * C], qkv_psum_b)

            def b_qkv(t):
                ps = ps_b[t.half]
                wait(act, qkv_psum_b, t.n + 1)
                wait(act, c_ready, t.n - 1)
                nc.scalar.activation(qkv_b[:, t.half].rearrange("p h s d -> p (h s d)"), ps[:, 0:3 * C],
                                     ACT.Copy).then_inc(qkv_ready_b, 1)

            def b_softmax(t):
                wait(act, s_low_ready, t.n + 1)
                wait(act, c_raw_ready[1], t.n - 1)
                nc.scalar.activation(p_b[:, t.half], s_low[:, t.half], ACT.Exp, scale=SCALE
                                     ).then_inc(p_ready, 1)

            def b_turn_out(t):
                wait(act, cT_psum, t.n + 1)
                wait(act, y_psum["b"], t.n - 1)
                nc.scalar.activation(cT_b[:, t.half, :], ps_b[t.half][:, 3 * C:4 * C], ACT.Copy
                                     ).then_inc(cT_ready, 1)

            walk(act, T, {"a_norm": norm("a"), "a_turn": a_turn, "a_qkv": a_qkv, "a_gram": a_gram,
                          "a_exp": a_exp, "a_spread": a_spread, "f1_norm": norm("f1"), "f1_turn": turn("f1"),
                          "f1_up": up("f1"), "f2_norm": norm("f2"), "f2_turn": turn("f2"), "f2_up": up("f2"),
                          "b_norm": norm("b"), "b_turn": b_turn, "b_qkv": b_qkv, "b_softmax": b_softmax,
                          "b_turn_out": b_turn_out})

        @block.vector
        def _(dve):
            dve.wait_ge(bias_in, 16 * len(BIAS))
            dve.wait_ge(zeros_ready, 2)
            steps = 0
            src = bias32
            for k in range(3):
                nc.vector.tensor_copy(bias_part[:, k, :], src[:, :]).then_inc(bias_steps, 1)
                steps += 1
                dve.wait_ge(bias_steps, steps)
                row = slice(QUAD * k, QUAD * k + 1)
                last = nc.vector.tensor_copy(bias[row, :], bias_part[row, k, :])
                if k < 2:
                    nc.vector.tensor_tensor(bias_rest[:, :], src[:, :], bias_part[:, k, :],
                                            ALU.subtract).then_inc(bias_steps, 1)
                    steps += 1
                    dve.wait_ge(bias_steps, steps)
                    src = bias_rest
            last.then_inc(bias_ready, 1)

            def alone(eng):
                eng.wait_ge(zeros_ready, 1)

            def statistics(k, t):
                src = xw if k == "a" else xs[LN_IN[k]]
                if k != "a":
                    alone(dve)
                    wait(dve, x_ready[LN_IN[k]], t.n + 1)
                elif isinstance(t.n, int) and t.n in (0, n_early):
                    i = int(t.n > 0)
                    dve.wait_ge(xw_in[i], windows_loads[i])
                h = t.half
                nc.vector.bn_stats(sums[k][:, h, :], src[:, t.n, :]).then_inc(ln_sums[k], 1)
                wait(dve, ln_sums[k], t.n + 1)
                nc.vector.memset(wait_carrier[:, :], 0.0)
                nc.vector.bn_aggr(mv[k][:, h, :], sums[k][:, h, :]).then_inc(ln_mv[k], 1)
                wait(dve, ln_mv[k], t.n + 1)
                wait(dve, ln_ready[k], t.n - 1)
                nc.vector.tensor_scalar_add(spread[k][:, h, :], mv[k][:, h, 1:2], EPS).then_inc(ln_spread[k], 1)

            def add_residual(k, t, src, dst, psum):
                wait(dve, y_psum[k], t.n + 1)
                if k == "a" and isinstance(t.n, int) and t.n == 0:
                    dve.wait_ge(x_in, 16 * GROUPS)
                nc.vector.tensor_tensor(xs[dst][:, t.n, :], psum, xs[src][:, t.n, :], ALU.add
                                        ).then_inc(x_ready[dst], 1)

            def norm(k):
                return lambda t: statistics(k, t)

            def a_logits(t):
                h = t.half
                wait(dve, gram_own_ready, t.n + 1)
                nc.vector.tensor_reduce(logit[:, :, :], gram_own[:, h].rearrange("p n h e -> p n e h"),
                                        AX_X, ALU.add).then_inc(logit_ready, 1)
                wait(dve, logit_ready, t.n + 1)
                nc.vector.tensor_reduce(logit_max[:, :], logit[:, :, :], AX_X, ALU.max
                                        ).then_inc(logit_max_ready, 1)
                wait(dve, logit_max_ready, t.n + 1)
                wait(dve, e_ready_a, t.n - 1)
                nc.vector.tensor_tensor(logit_low[:, h], logit[:, :, :],
                                        logit_max[:, :].unsqueeze(2).broadcast_to([P, NW, HD]),
                                        ALU.subtract).then_inc(logit_low_ready, 1)

            def a_sums(t):
                h = t.half
                wait(dve, e_ready_a, t.n + 1)
                nc.vector.tensor_reduce(e_sum_a[:, :], e_a[:, h], AX_X, ALU.add).then_inc(e_sum_ready_a, 1)
                wait(dve, e_sum_ready_a, t.n + 1)
                nc.vector.reciprocal(e_inv_a[:, h, :], e_sum_a[:, :]).then_inc(e_inv_ready_a, 1)

            def a_context(t):
                wait(dve, o_psum, t.n + 1)
                wait(dve, e_inv_ready_a, t.n + 1)
                wait(dve, o_wide_ready, t.n - 1)
                nc.vector.tensor_tensor(
                    o_a[:, t.half].rearrange("p (j n) c -> p n j c", n=NW),
                    ps_out[:, 0:P].rearrange("p (n j c) -> p n j c", n=NW, j=GROUPS),
                    e_inv_a[:, t.half, :].unsqueeze(2).unsqueeze(3).broadcast_to([P, NW, GROUPS, HD]),
                    ALU.mult).then_inc(o_ready, 1)

            def a_turn_out(t):
                wait(dve, o_wide_ready, t.n + 1)
                wait(dve, y_psum["a"], t.n - 1)
                nc.vector.transpose(o_turned[:, t.half].rearrange("p h m d -> p m h d"),
                                    o_wide[:, t.half]).then_inc(o_turned_ready, 1)

            def a_project(t):
                add_residual("a", t, 0, 1, ps_out[:, C:2 * C])

            def down(k):
                return lambda t: add_residual(k, t, *FFN[k], ps_f[k][:, 0:C])

            def b_qk(j):
                def run(t):
                    k = ps_b[t.half][:, 0:3 * C].rearrange("p (h s d) -> p h s d", s=3, d=HD)[:, :, 1, :]
                    wait(dve, qkv_ready_b, t.n + 1)
                    nc.vector.tensor_tensor(qk[:, MADE[j]], *q_times_k(t, k, MADE[j]), ALU.mult
                                            ).then_inc(qk_ready_b[j], 1)
                return run

            def b_s(j):
                def run(t):
                    wait(dve, qk_ready_b[j], t.n + 1)
                    if j == 1:
                        wait(dve, qk_ready_pool, t.n + 1)
                    nc.vector.tensor_reduce(s_b[:, SUMMED[j], :], qk[:, SUMMED[j]], AX_X, ALU.add
                                            ).then_inc(s_ready[j], 1)
                return run

            def b_softmax(t):
                h = t.half
                for j in range(2):
                    wait(dve, s_ready[j], t.n + 1)
                nc.vector.tensor_reduce(s_max[:, :], s_b[:, :, :], AX_X, ALU.max).then_inc(s_max_ready, 1)
                wait(dve, s_max_ready, t.n + 1)
                wait(dve, p_ready, t.n - 1)
                nc.vector.tensor_tensor(s_low[:, h], s_b[:, :, :],
                                        s_max[:, :].unsqueeze(2).broadcast_to([P, HEADS, HEADS]),
                                        ALU.subtract).then_inc(s_low_ready, 1)

            def b_pv(j):
                def run(t):
                    v = ps_b[t.half][:, 0:3 * C].rearrange("p (h s d) -> p d s h", s=3, d=HD)[:, :, 2, :]
                    wait(dve, p_ready, t.n + 1)
                    nc.vector.tensor_tensor(pv[:, MADE[j]], *v_times_p(t, v, MADE[j]), ALU.mult
                                            ).then_inc(pv_ready[j], 1)
                return run

            def b_sums(t):
                nc.vector.tensor_reduce(p_sum[:, :], p_b[:, t.half], AX_X, ALU.add).then_inc(p_sum_ready, 1)

            def b_c(j):
                def run(t):
                    wait(dve, pv_ready[j], t.n + 1)
                    if j == 1:
                        wait(dve, pv_ready_pool, t.n + 1)
                    nc.vector.tensor_reduce(c_raw[:, SUMMED[j], :], pv[:, SUMMED[j]], AX_X, ALU.add
                                            ).then_inc(c_raw_ready[j], 1)
                    if j == 0:
                        wait(dve, p_sum_ready, t.n + 1)
                        nc.vector.reciprocal(p_inv[:, :], p_sum[:, :]).then_inc(p_inv_ready, 1)
                return run

            def b_scale(t):
                wait(dve, p_inv_ready, t.n + 1)
                for i in range(2):
                    wait(dve, c_raw_ready[i], t.n + 1)
                wait(dve, cT_psum, t.n - 1)
                nc.vector.tensor_tensor(c_b[:, t.half], c_raw[:, :, :],
                                        p_inv[:, :].unsqueeze(2).broadcast_to([P, HEADS, HD]),
                                        ALU.mult).then_inc(c_ready, 1)

            def b_project(t):
                add_residual("b", t, 2, 3, ps_b[t.half][:, 0:C])

            walk(dve, T, {"a_norm": norm("a"), "a_logits": a_logits, "a_sums": a_sums,
                          "a_context": a_context, "a_turn_out": a_turn_out, "a_project": a_project,
                          "f1_norm": norm("f1"), "f1_down": down("f1"), "f2_norm": norm("f2"),
                          "f2_down": down("f2"), "b_norm": norm("b"), "b_qk_0": b_qk(0), "b_qk_1": b_qk(1),
                          "b_s_0": b_s(0), "b_s_1": b_s(1), "b_softmax": b_softmax, "b_sums": b_sums,
                          "b_pv_0": b_pv(0), "b_pv_1": b_pv(1), "b_c_0": b_c(0), "b_c_1": b_c(1),
                          "b_scale": b_scale, "b_project": b_project})

        @block.tensor
        def _(pe):
            pe.wait_ge(ident_ready, 1)
            pe.wait_ge(ones_ready, 1)

            def mm(psum, lhsT, rhs, start=False, stop=False):
                return nc.tensor.matmul(psum, lhsT, rhs, start=start, stop=stop)

            def turn_in(k, t, psum):
                wait(pe, xn_ready[k], t.n + 1)
                nc.tensor.transpose(psum, xn[k][:, t.half, :], ident[:, :]).then_inc(xnT_psum[k], 1)

            def first(t):
                return isinstance(t.n, int) and t.n == 0

            def a_turn(t):
                wait(pe, v_ready_a, t.n)
                turn_in("a", t, ps_in[:, 3 * C:4 * C])

            def a_qkv(t):
                wait(pe, xnT_ready["a"], t.n + 1)
                if first(t):
                    pe.wait_ge(w_in["a_qkv"], 16)
                    pe.wait_ge(bias_ready, 1)
                xT = xnT["a"][:, t.half, :]
                b = bias[:, bias_at["a_qkv"]]
                mm(ps_in[:, 0:2 * C], xT, wqkv_a[:, 0:2 * C], start=True)
                mm(ps_in[:, 0:2 * C], ones[:, :], b[:, 0:2 * C], stop=True)
                mm(ps_in[:, 2 * C:3 * C], wqkv_a[:, 2 * C:3 * C], xT, start=True)
                mm(ps_in[:, 2 * C:3 * C], b[:, 2 * C:3 * C], ones[:, :], stop=True).then_inc(qkv_psum_a, 1)

            def a_gram(t):
                wait(pe, qk_ready_a, t.n + 1)
                wait(pe, gram_ready, t.n)
                mm(ps_gram[:, :], q_a[:, t.half, :], k_a[:, t.half].rearrange("p n c -> p (n c)"),
                   start=True, stop=True).then_inc(gram_psum, 1)

            def a_spread(t):
                wait(pe, e_diag_ready, t.n + 1)
                wait(pe, eT_ready, t.n)
                for n in range(NW):
                    last = nc.tensor.transpose(ps_eT[:, P * n:P * (n + 1)],
                                               e_diag[:, t.half, n].rearrange("p h e -> p (h e)"), ident[:, :])
                last.then_inc(eT_psum, 1)

            def a_context(t):
                wait(pe, eT_ready, t.n + 1)
                wait(pe, v_ready_a, t.n + 1)
                wait(pe, x_ready[1], t.n)
                for n in range(NW):
                    cols = slice(WIN * n, WIN * (n + 1))
                    last = mm(ps_out[:, cols], eT[:, t.half, n, :], vT_a[:, t.half, cols], start=True, stop=True)
                last.then_inc(o_psum, 1)

            def a_project(t):
                wait(pe, o_turned_ready, t.n + 1)
                wait(pe, o_ready, t.n + 1)
                if first(t):
                    pe.wait_ge(w_in["a_out"], 16)
                for i in range(HQ):
                    mm(ps_out[:, C:2 * C], o_turned[:, t.half, i].rearrange("p m d -> p (m d)"),
                       wout_a[:, :], start=i == 0)
                mm(ps_out[:, C:2 * C], ones[:, :], bias[:, bias_at["a_out"]], stop=True
                   ).then_inc(y_psum["a"], 1)

            def turn(k):
                def run(t):
                    wait(pe, x_ready[FFN[k][1]], t.n)
                    turn_in(k, t, ps_f[k][:, 0:P])
                return run

            def up(k):
                def run(t):
                    if first(t):
                        pe.wait_ge(w_in["f"], 32)
                    wait(pe, xnT_ready[k], t.n + 1)
                    for i in range(NF):
                        cols = slice(P * i, P * (i + 1))
                        mm(ps_f[k][:, cols], w1[:, cols], xnT[k][:, t.half, :], start=True)
                        last = mm(ps_f[k][:, cols], bias[:, bias_at["f1"]][:, cols], ones[:, :], stop=True)
                    last.then_inc(h_psum[k], 1)
                return run

            def down(k):
                def run(t):
                    wait(pe, h_ready[k], t.n + 1)
                    for i in range(NF):
                        mm(ps_f[k][:, 0:C], hT[k][:, t.half, i, :], w2[:, i, :], start=i == 0)
                    mm(ps_f[k][:, 0:C], ones[:, :], bias[:, bias_at["f2"]], stop=True).then_inc(y_psum[k], 1)
                return run

            def b_turn(t):
                wait(pe, x_ready[3], t.n - 1)
                turn_in("b", t, ps_b[t.half][:, 3 * C:4 * C])

            def b_qkv(t):
                ps = ps_b[t.half]
                if first(t):
                    pe.wait_ge(w_in["b"], 32)
                wait(pe, xnT_ready["b"], t.n + 1)
                mm(ps[:, 0:3 * C], xnT["b"][:, t.half, :], wqkv_b[:, :], start=True)
                mm(ps[:, 0:3 * C], ones[:, :], bias[:, bias_at["b_qkv"]], stop=True).then_inc(qkv_psum_b, 1)

            def b_turn_out(t):
                ps = ps_b[t.half]
                wait(pe, c_ready, t.n + 1)
                nc.tensor.transpose(ps[:, 3 * C:4 * C], c_b[:, t.half].rearrange("p h d -> p (h d)"),
                                    ident[:, :]).then_inc(cT_psum, 1)

            def b_project(t):
                ps = ps_b[t.half]
                wait(pe, cT_ready, t.n + 1)
                mm(ps[:, 0:C], cT_b[:, t.half, :], wout_b[:, :], start=True)
                mm(ps[:, 0:C], ones[:, :], bias[:, bias_at["b_out"]], stop=True).then_inc(y_psum["b"], 1)

            walk(pe, T, {"a_turn": a_turn, "a_qkv": a_qkv, "a_gram": a_gram, "a_spread": a_spread,
                         "a_context": a_context, "a_project": a_project, "f1_turn": turn("f1"),
                         "f1_up": up("f1"), "f1_down": down("f1"), "f2_turn": turn("f2"), "f2_up": up("f2"),
                         "f2_down": down("f2"), "b_turn": b_turn, "b_qkv": b_qkv,
                         "b_turn_out": b_turn_out, "b_project": b_project})


_INS = ["L0_attn_a_x", "L0_attn_a_W_qkv", "L0_attn_a_b_qkv", "L0_attn_a_W_out", "L0_attn_a_b_out",
        "L0_attn_b_W_qkv", "L0_attn_b_b_qkv", "L0_attn_b_W_out", "L0_attn_b_b_out",
        "L0_ffn_w1", "L0_ffn_b1", "L0_ffn_w2", "L0_ffn_b2"]


def kernel(**inputs):
    import numpy as _np
    import concourse.bacc as _bacc
    from concourse import mybir as _mybir
    from concourse.bass_utils import run_bass_kernel_spmd as _run

    nc = _bacc.Bacc("TRN2", target_bir_lowering=False, num_devices=1)
    arrays, args = {}, []
    for name in _INS:
        a = _np.ascontiguousarray(inputs[name])
        arrays[f"in_{name}_dram"] = a
        args.append(nc.dram_tensor(f"in_{name}_dram", a.shape, _mybir.dt.from_np(a.dtype),
                                   kind="ExternalInput").ap())
    shape = inputs["L0_attn_a_x"].shape
    args.append(nc.dram_tensor("out_0_dram", shape, _mybir.dt.float32, kind="ExternalOutput").ap())
    hybrid_block(nc, *args)
    r = _run(nc, [arrays], core_ids=[0])
    return r.results[0]["out_0_dram"]
```

```python
from contextlib import ExitStack

import concourse.bass as bass
from concourse import mybir

P = 128
F32 = mybir.dt.float32
BF16 = mybir.dt.bfloat16
ALU = mybir.AluOpType
ACT = mybir.ActivationFunctionType
AX_X = mybir.AxisListType.X

HEADS = 16
HD = 8
WIN = 32
HOP = WIN // 2
EPS = 1e-5
SCALE = float(HD) ** -0.5
QUAD = 32
HQ = QUAD // HD
ROWS_PER_WIN = WIN
NW = P // ROWS_PER_WIN
GROUPS = WIN // HD

STEP = [("b_xn", 5), ("a_gram", 2), ("b_max", 6), ("a_sums", 3), ("b_softmax", 6), ("b_project", 7),
        ("f1_xn", 4), ("a_stats", 0), ("f2_stats", 7), ("a_context", 3), ("b_pv", 6), ("b_turn", 5),
        ("a_xn", 1), ("f2_norm", 7), ("b_sums", 6), ("a_turn_out", 3), ("f1_turn", 4), ("f2_xn", 8),
        ("b_qkv", 5), ("a_logits", 2), ("a_turn", 1), ("b_c_own", 6), ("b_pv_pool", 6), ("b_inv", 6),
        ("b_qk", 5), ("f2_turn", 8), ("f1_up", 4), ("f2_up", 8), ("b_c_pool", 6), ("a_project", 3),
        ("b_s_own", 5), ("b_qk_pool", 5), ("f1_down", 4), ("f1_stats", 3), ("b_scale", 6),
        ("b_stats", 4), ("a_norm", 0), ("a_exp", 2), ("f1_norm", 3), ("b_norm", 4), ("b_s_pool", 5),
        ("a_qkv", 1), ("b_turn_out", 6), ("f2_down", 8), ("a_spread", 2), ("ln", 0)]
LAG = max(d for _, d in STEP)

LN = ("a", "f1", "b", "f2")
LN_LAG = {k: dict(STEP)[k + "_norm"] for k in LN}

OWN_QK, POOL_QK = slice(0, 5), slice(5, HEADS)
OWN_PV, POOL_PV = slice(0, 5), slice(5, HEADS)


class Tile:

    def __init__(self, n, half):
        self.n, self.half = n, half


def wait(eng, sem, count):
    if isinstance(count, int) and count <= 0:
        return
    eng.wait_ge(sem, count)


def walk(eng, tiles, stages):
    def at(s):
        for name, lag in STEP:
            if name in stages and 0 <= s - lag < tiles + (max(LN_LAG.values()) if name == "ln" else 0):
                stages[name](Tile(s - lag, (s - lag) % 2))

    begin = LAG + 2
    for s in range(begin):
        at(s)
    with eng.Fori(0, (tiles - begin) // 2) as pair:
        for odd in range(2):
            for name, lag in STEP:
                if name in stages:
                    stages[name](Tile(pair * 2 + (begin + odd - lag), (begin + odd - lag) % 2))
    for s in range(begin + (tiles - begin) // 2 * 2, tiles + LAG):
        at(s)


def hybrid_block(nc, x, a_wqkv, a_bqkv, a_wout, a_bout, b_wqkv, b_bqkv, b_wout, b_bout,
                 f_w1, f_b1, f_w2, f_b2, out):
    B, L, C = x.shape
    FF = f_w1.shape[1]
    NF = FF // P
    TPB = L // P
    T = B * TPB
    assert C == P == HEADS * HD and NF * P == 512
    HOP_T = NW * HOP
    assert (L - P) // P * HOP_T + (NW - 1) * HOP + WIN <= L

    with ExitStack() as ctx:
        def sb(name, shape, dt=F32):
            return ctx.enter_context(nc.sbuf_tensor(name, shape, dt))

        def sem(name):
            return ctx.enter_context(nc.semaphore(name))

        xw = sb("xw", [P, T, C])
        xs = [sb(f"x{i}", [P, T, C]) for i in range(5)]
        wqkv_a, wout_a = sb("wqkv_a", [P, 3 * C]), sb("wout_a", [P, C])
        wout_one = sb("wout_one", [P, HQ, C])
        wqkv_b, wout_b = sb("wqkv_b", [P, 3 * C]), sb("wout_b", [P, C])
        w1, w2 = sb("w1", [P, FF]), sb("w2", [P, NF, C])
        BIAS = [("a_qkv", a_bqkv, 3 * C), ("a_out", a_bout, C), ("f1", f_b1, FF), ("f2", f_b2, C),
                ("b_qkv", b_bqkv, 3 * C), ("b_out", b_bout, C)]
        nb = sum(n for _, _, n in BIAS)
        PARTS = 3
        bias32 = sb("bias32", [nb // P, P])
        bias_rest = sb("bias_rest", [nb // P, P])
        bias_part = sb("bias_part", [nb // P, PARTS, P], BF16)
        bias = sb("bias", [PARTS, nb], BF16)
        bias_up = sb("bias_up", [PARTS * NF, P], BF16)
        chunk_of = sb("chunk_of", [PARTS * NF, NF, P], BF16)
        at, bias_at = 0, {}
        for name, _, n in BIAS:
            bias_at[name] = slice(at, at + n)
            at += n
        ones = sb("ones", [PARTS, P], BF16)
        wait_carrier = sb("wait_carrier", [P, len(LN)])
        minus_one, minus_half, eps = (
            sb(name, [P, len(LN)]) for name in ("minus_one", "minus_half", "eps"))
        ident = sb("ident", [P, P])
        head_mask = sb("head_mask", [P, HEADS, HD])
        quad_mask = sb("quad_mask", [P, HQ, HD])

        sums = {k: sb(f"sums_{k}", [P, 2, 6]) for k in LN}
        mv = sb("mv", [P, 2, len(LN), 2])
        spread = sb("spread", [P, 2, len(LN)])
        minus = sb("minus", [P, 2, len(LN)])
        rstd = sb("rstd", [P, 2, len(LN)])
        shift = sb("shift", [P, 2, len(LN)])
        xn = {k: sb(f"xn_{k}", [P, 2, C]) for k in LN}
        xnT = {k: sb(f"xnT_{k}", [P, 2, P]) for k in LN}

        q_a = sb("q_a", [P, 2, C])
        k_a = sb("k_a", [P, 2, NW, C])
        vT_a = sb("vT_a", [P, 2, P])
        gram = sb("gram", [P, 2, NW, HQ, HD])
        gram_own = sb("gram_own", [P, 2, NW, HQ, HD])
        logit = sb("logit", [P, NW, HD])
        logit_max = sb("logit_max", [P, NW])
        logit_low = sb("logit_low", [P, 2, NW, HD])
        e_a = sb("e_a", [P, 2, NW, HD])
        e_sum_a = sb("e_sum_a", [P, NW])
        e_inv_a = sb("e_inv_a", [P, 2, NW])
        e_diag = sb("e_diag", [P, 2, NW, HEADS, HD])
        eT = sb("eT", [P, 2, NW, P])
        o_a = sb("o_a", [P, 2, NW * GROUPS, HD])
        o_turned = sb("o_turned", [P, 2, HQ, NW * GROUPS, HD])

        hT = {k: sb(f"hT_{k}", [P, 2, NF, P]) for k in ("f1", "f2")}

        qkv_b = sb("qkv_b", [P, 2, HEADS, 3, HD])
        qk = sb("qk", [P, 2, HEADS, HEADS, HD])
        pv = sb("pv", [P, 2, HEADS, HD, HEADS])
        s_b = sb("s_b", [P, HEADS, HEADS])
        s_max = sb("s_max", [P, HEADS])
        s_low = sb("s_low", [P, 2, HEADS, HEADS])
        p_b = sb("p_b", [P, 2, HEADS, HEADS])
        p_sum = sb("p_sum", [P, HEADS])
        p_inv = sb("p_inv", [P, HEADS])
        c_raw = sb("c_raw", [P, HEADS, HD])
        c_b = sb("c_b", [P, 2, HEADS, HD])
        cT_b = sb("cT_b", [P, 2, P])

        def bank(name):
            return ctx.enter_context(nc.psum_tensor(name, [P, 512], F32))

        ps_in, ps_gram, ps_eT, ps_out = bank("ps_in"), bank("ps_gram"), bank("ps_eT"), bank("ps_out")
        ps_f = {k: bank(f"ps_{k}") for k in ("f1", "f2")}
        ps_b_in, ps_b_out = bank("ps_b_in"), bank("ps_b_out")

        n_early = 2
        xw_in = [sem("xw_first_in"), sem("xw_rest_in")]
        windows_loads = [16 * NW, 16 * NW * B]
        x_in = sem("x_in")
        w_in = {k: sem(f"w_{k}_in") for k in ("a_qkv", "a_out", "f", "b")}
        bias_in = sem("bias_in")
        bias_steps, bias_parts_ready, bias_ready = (
            sem("bias_steps"), sem("bias_parts_ready"), sem("bias_ready"))
        chunks_ready = sem("chunks_ready")
        const_steps, scalars_ready = sem("const_steps"), sem("scalars_ready")
        ident_ready, masks_ready = sem("ident_ready"), sem("masks_ready")
        zeros_ready, ones_ready = sem("zeros_ready"), sem("ones_ready")
        ln_sums = {k: sem(f"ln_sums_{k}") for k in LN}
        ln_mv = {k: sem(f"ln_mv_{k}") for k in LN}
        mv_zeros_ready = sem("mv_zeros_ready")
        ln_spread, ln_rstd, ln_ready = sem("ln_spread"), sem("ln_rstd"), sem("ln_ready")
        xn_ready = {k: sem(f"xn_ready_{k}") for k in LN}
        xnT_psum = {k: sem(f"xnT_psum_{k}") for k in LN}
        xnT_ready = {k: sem(f"xnT_ready_{k}") for k in LN}
        x_ready = [x_in] + [sem(f"x{i}_ready") for i in range(1, 5)]
        qkv_psum_a, qk_ready_a, v_ready_a = sem("qkv_psum_a"), sem("qk_ready_a"), sem("v_ready_a")
        gram_psum, gram_ready, gram_own_ready = sem("gram_psum"), sem("gram_ready"), sem("gram_own_ready")
        logit_ready, logit_max_ready, logit_low_ready = (
            sem("logit_ready"), sem("logit_max_ready"), sem("logit_low_ready"))
        e_ready_a, e_sum_ready_a, e_inv_ready_a = sem("e_ready_a"), sem("e_sum_ready_a"), sem("e_inv_ready_a")
        e_diag_ready, eT_psum, eT_ready = sem("e_diag_ready"), sem("eT_psum"), sem("eT_ready")
        o_psum, o_ready, o_turned_ready = sem("o_psum"), sem("o_ready"), sem("o_turned_ready")
        w_out_ready = sem("w_out_ready")
        y_psum = {k: sem(f"y_psum_{k}") for k in LN}
        h_psum = {k: sem(f"h_psum_{k}") for k in ("f1", "f2")}
        h_ready = {k: sem(f"h_ready_{k}") for k in ("f1", "f2")}
        qkv_psum_b, qkv_ready_b = sem("qkv_psum_b"), sem("qkv_ready_b")
        qk_ready_own, pv_ready_own = sem("qk_ready_own"), sem("pv_ready_own")
        qk_ready_pool, pv_ready_pool = sem("qk_ready_pool"), sem("pv_ready_pool")
        s_ready_own, s_ready_pool = sem("s_ready_own"), sem("s_ready_pool")
        s_max_ready, s_low_ready, p_ready = sem("s_max_ready"), sem("s_low_ready"), sem("p_ready")
        p_sum_ready, p_inv_ready = sem("p_sum_ready"), sem("p_inv_ready")
        c_ready_own, c_ready_pool = sem("c_ready_own"), sem("c_ready_pool")
        c_ready, cT_psum, cT_ready = sem("c_ready"), sem("cT_psum"), sem("cT_ready")
        out_stored = sem("out_stored")

        LN_IN = {"a": None, "f1": 1, "b": 2, "f2": 3}
        FFN = {"f1": (1, 2), "f2": (3, 4)}

        x_rows = x.rearrange("b (i m j) c -> j m (b i) c", j=GROUPS, m=P // GROUPS)
        out_rows = out.rearrange("b (i m j) c -> (b i) j m c", j=GROUPS, m=P // GROUPS)

        def q_times_k(t, heads):
            shape = [P, heads.stop - heads.start, HEADS, HD]
            return (qkv_b[:, t.half, :, 1, :].unsqueeze(1).broadcast_to(shape),
                    qkv_b[:, t.half, heads, 0, :].unsqueeze(2).broadcast_to(shape))

        def v_times_p(t, heads):
            shape = [P, heads.stop - heads.start, HD, HEADS]
            return (qkv_b[:, t.half, :, 2, :].rearrange("p h d -> p d h").unsqueeze(1).broadcast_to(shape),
                    p_b[:, t.half, heads, :].unsqueeze(2).broadcast_to(shape))

        block = ctx.enter_context(nc.Block())

        @block.sync
        def _(sp):
            def load_windows(first, last, done):
                for b in range(B):
                    lo, hi = max(first, b * TPB), min(last, (b + 1) * TPB)
                    if lo >= hi:
                        continue
                    for n in range(NW):
                        at = (lo - b * TPB) * HOP_T + n * HOP
                        src = x[b, at:at + WIN, :]
                        src = bass.AP(src.tensor, src.offset, [[C, WIN], [HOP_T * C, hi - lo], [1, C]])
                        sp.dma_start(xw[WIN * n:WIN * (n + 1), lo:hi, :], src).then_inc(done, 16)

            load_windows(0, n_early, xw_in[0])
            sp.dma_start(wqkv_a[:, :], a_wqkv).then_inc(w_in["a_qkv"], 16)
            load_windows(n_early, T, xw_in[1])
            sp.wait_ge(bias_parts_ready, 1)
            up_rows = slice(bias_at["f1"].start // P, bias_at["f1"].stop // P)
            for k in range(PARTS):
                sp.dma_start(bias[k:k + 1, :].rearrange("a (r n) -> a r n", n=P),
                              bias_part[:, k, :]).then_inc(bias_ready, 16)
                sp.dma_start(bias_up[NF * k:NF * (k + 1), :], bias_part[up_rows, k, :]).then_inc(bias_ready, 16)
            sp.dma_start(wout_a[:, :], a_wout).then_inc(w_in["a_out"], 16)
            for j in range(GROUPS):
                sp.dma_start(xs[0][P // GROUPS * j:P // GROUPS * (j + 1), :, :], x_rows[j]).then_inc(x_in, 16)
            sp.dma_start(w1[:, :], f_w1).then_inc(w_in["f"], 16)
            sp.dma_start(w2[:, :, :], f_w2.rearrange("(k p) c -> p k c", p=P)).then_inc(w_in["f"], 16)
            sp.dma_start(wqkv_b[:, :], b_wqkv).then_inc(w_in["b"], 16)
            sp.dma_start(wout_b[:, :], b_wout).then_inc(w_in["b"], 16)

            def store(t):
                wait(sp, x_ready[4], t.n + 1)
                sp.dma_start(out_rows[t.n], xs[4][:, t.n, :]).then_inc(out_stored, 16)

            with sp.Fori(0, T) as t:
                store(Tile(t, None))
            sp.wait_ge(out_stored, 16 * T)

        @block.gpsimd
        def _(pool):
            nc.gpsimd.memset(ident[:, :], 0.0).then_inc(const_steps, 1)
            nc.gpsimd.memset(head_mask[:, :, :], 1.0).then_inc(const_steps, 1)
            nc.gpsimd.memset(ones[:, :], 1.0).then_inc(ones_ready, 1)
            nc.gpsimd.memset(chunk_of[:, :, :], 0.0).then_inc(chunks_ready, 1)
            nc.gpsimd.memset(minus_one[:, :], -1.0).then_inc(scalars_ready, 1)
            nc.gpsimd.memset(minus_half[:, :], -0.5).then_inc(scalars_ready, 1)
            nc.gpsimd.memset(eps[:, :], EPS).then_inc(scalars_ready, 1)
            pool.wait_ge(const_steps, 2)
            nc.gpsimd.affine_select(out=ident[:, :], in_=ident[:, :], compare_op=ALU.not_equal, fill=1.0,
                                    base=0, pattern=[[-1, P]], channel_multiplier=1).then_inc(ident_ready, 1)
            nc.gpsimd.affine_select(out=head_mask[:, :, :], in_=head_mask[:, :, :], compare_op=ALU.is_ge,
                                    fill=0.0, base=0, pattern=[[-HD, HEADS], [0, HD]],
                                    channel_multiplier=1).then_inc(const_steps, 1)
            pool.wait_ge(const_steps, 3)
            nc.gpsimd.affine_select(out=head_mask[:, :, :], in_=head_mask[:, :, :], compare_op=ALU.is_ge,
                                    fill=0.0, base=HD - 1, pattern=[[HD, HEADS], [0, HD]],
                                    channel_multiplier=-1).then_inc(const_steps, 1)
            for k in range(PARTS):
                pool.wait_ge(chunks_ready, k + 1)
                nc.gpsimd.affine_select(out=chunk_of[:, :, :], in_=chunk_of[:, :, :],
                                        compare_op=ALU.not_equal, fill=1.0, base=-NF * k,
                                        pattern=[[-1, NF], [0, P]], channel_multiplier=1).then_inc(chunks_ready, 1)
            pool.wait_ge(scalars_ready, 3)
            pool.wait_ge(mv_zeros_ready, 1)
            pool.wait_ge(masks_ready, 1)

            def ln(s):
                def tile_count(k, more):
                    count = s.n - LN_LAG[k] + more
                    return min(count, T) if isinstance(count, int) else count

                h = s.half
                for k in LN:
                    wait(pool, ln_mv[k], tile_count(k, 1))
                    wait(pool, xn_ready[k], tile_count(k, -1))
                nc.gpsimd.tensor_tensor(spread[:, h], mv[:, h, :, 1], eps[:, :], ALU.add).then_inc(ln_spread, 1)
                nc.gpsimd.tensor_tensor(minus[:, h], mv[:, h, :, 0], minus_one[:, :], ALU.mult)
                wait(pool, ln_spread, s.n + 1)
                nc.gpsimd.tensor_tensor(rstd[:, h], spread[:, h], minus_half[:, :], ALU.pow
                                        ).then_inc(ln_rstd, 1)
                wait(pool, ln_rstd, s.n + 1)
                nc.gpsimd.tensor_tensor(shift[:, h], minus[:, h], rstd[:, h], ALU.mult).then_inc(ln_ready, 1)

            def a_logits(t):
                wait(pool, gram_ready, t.n + 1)
                wait(pool, logit_ready, t.n - 1)
                nc.gpsimd.tensor_tensor(gram_own[:, t.half], gram[:, t.half],
                                        quad_mask[:, :, :].unsqueeze(1).broadcast_to([P, NW, HQ, HD]),
                                        ALU.mult).then_inc(gram_own_ready, 1)

            def a_spread(t):
                wait(pool, e_ready_a, t.n + 1)
                wait(pool, eT_psum, t.n - 1)
                nc.gpsimd.tensor_tensor(
                    e_diag[:, t.half],
                    e_a[:, t.half].unsqueeze(2).broadcast_to([P, NW, HEADS, HD]),
                    head_mask[:, :, :].unsqueeze(1).broadcast_to([P, NW, HEADS, HD]),
                    ALU.mult).then_inc(e_diag_ready, 1)

            def b_qk_pool(t):
                wait(pool, qkv_ready_b, t.n + 1)
                wait(pool, s_ready_pool, t.n - 1)
                nc.gpsimd.tensor_tensor(qk[:, t.half, POOL_QK], *q_times_k(t, POOL_QK), ALU.mult).then_inc(qk_ready_pool, 1)

            def b_pv_pool(t):
                wait(pool, p_ready, t.n + 1)
                wait(pool, c_ready_pool, t.n - 1)
                nc.gpsimd.tensor_tensor(pv[:, t.half, POOL_PV], *v_times_p(t, POOL_PV), ALU.mult).then_inc(pv_ready_pool, 1)

            walk(pool, T, {"ln": ln, "a_logits": a_logits, "a_spread": a_spread,
                           "b_qk_pool": b_qk_pool, "b_pv_pool": b_pv_pool})

        @block.scalar
        def _(act):
            at = 0
            for name, b, n in BIAS:
                act.dma_start(bias32[at // P:(at + n) // P, :], b.rearrange("(a n) -> a n", n=P)
                              ).then_inc(bias_in, 16)
                at += n

            act.wait_ge(const_steps, 4)
            for g in range(P // QUAD):
                rows = slice(QUAD * g, QUAD * (g + 1))
                last = nc.scalar.activation(quad_mask[rows, :, :], head_mask[rows, HQ * g:HQ * (g + 1), :],
                                            ACT.Copy)
            last.then_inc(masks_ready, 1)

            def normalise(k, t):
                src = xw if k == "a" else xs[LN_IN[k]]
                i, h = LN.index(k), (t.half + LN_LAG[k]) % 2
                wait(act, ln_ready, t.n + LN_LAG[k] + 1)
                wait(act, xnT_psum[k], t.n - 1)
                nc.scalar.activation(xn[k][:, t.half, :], src[:, t.n, :], ACT.Identity,
                                     bias=shift[:, h, i:i + 1], scale=rstd[:, h, i:i + 1]
                                     ).then_inc(xn_ready[k], 1)

            def copy_xnT(k, t, psum, reader):
                wait(act, xnT_psum[k], t.n + 1)
                wait(act, reader, t.n - 1)
                nc.scalar.activation(xnT[k][:, t.half, :], psum, ACT.Copy).then_inc(xnT_ready[k], 1)

            def a_turn(t):
                copy_xnT("a", t, ps_in[:, 3 * C:4 * C], qkv_psum_a)

            def a_qkv(t):
                wait(act, qkv_psum_a, t.n + 1)
                wait(act, gram_psum, t.n - 1)
                if isinstance(t.n, int) and t.n == 0:
                    act.wait_ge(zeros_ready, 1)
                nc.scalar.activation(q_a[:, t.half, :], ps_in[:, 0:C], ACT.Copy)
                for n in range(NW):
                    rows = slice(WIN * n, WIN * (n + 1))
                    last = nc.scalar.activation(k_a[rows, t.half, n, :], ps_in[rows, C:2 * C], ACT.Copy)
                last.then_inc(qk_ready_a, 1)
                wait(act, o_psum, t.n - 1)
                nc.scalar.activation(vT_a[:, t.half, :], ps_in[:, 2 * C:3 * C], ACT.Copy
                                     ).then_inc(v_ready_a, 1)

            def a_gram(t):
                wait(act, gram_psum, t.n + 1)
                wait(act, gram_own_ready, t.n - 1)
                pg = ps_gram[:, :].rearrange("p (n c) -> p n c", n=NW)
                for g in range(P // QUAD):
                    rows = slice(QUAD * g, QUAD * (g + 1))
                    last = nc.scalar.activation(gram[rows, t.half].rearrange("p n h e -> p n (h e)"),
                                                pg[rows, :, rows], ACT.Copy)
                last.then_inc(gram_ready, 1)

            def a_exp(t):
                wait(act, logit_low_ready, t.n + 1)
                wait(act, e_inv_ready_a, t.n - 1)
                wait(act, e_diag_ready, t.n - 1)
                nc.scalar.activation(e_a[:, t.half], logit_low[:, t.half], ACT.Exp, scale=SCALE
                                     ).then_inc(e_ready_a, 1)

            def a_spread(t):
                wait(act, eT_psum, t.n + 1)
                wait(act, o_psum, t.n - 1)
                nc.scalar.activation(eT[:, t.half].rearrange("p n c -> p (n c)"), ps_eT[:, :], ACT.Copy
                                     ).then_inc(eT_ready, 1)

            def norm(k):
                return lambda t: normalise(k, t)

            def turn(k):
                return lambda t: copy_xnT(k, t, ps_f[k][:, 0:P], h_psum[k])

            def up(k):
                def run(t):
                    wait(act, h_psum[k], t.n + 1)
                    wait(act, y_psum[k], t.n - 1)
                    nc.scalar.activation(hT[k][:, t.half].rearrange("p k c -> p (k c)"), ps_f[k][:, :],
                                         ACT.Gelu).then_inc(h_ready[k], 1)
                return run

            def b_turn(t):
                copy_xnT("b", t, ps_b_in[:, 3 * C:4 * C], qkv_psum_b)

            def b_qkv(t):
                wait(act, qkv_psum_b, t.n + 1)
                wait(act, c_ready, t.n - 1)
                nc.scalar.activation(qkv_b[:, t.half].rearrange("p h s d -> p (h s d)"), ps_b_in[:, 0:3 * C],
                                     ACT.Copy).then_inc(qkv_ready_b, 1)

            def b_softmax(t):
                wait(act, s_low_ready, t.n + 1)
                wait(act, c_ready, t.n - 1)
                nc.scalar.activation(p_b[:, t.half], s_low[:, t.half], ACT.Exp, scale=SCALE
                                     ).then_inc(p_ready, 1)

            def b_turn_out(t):
                wait(act, cT_psum, t.n + 1)
                wait(act, y_psum["b"], t.n - 1)
                nc.scalar.activation(cT_b[:, t.half, :], ps_b_out[:, C:2 * C], ACT.Copy
                                     ).then_inc(cT_ready, 1)

            walk(act, T, {"a_xn": norm("a"), "a_turn": a_turn, "a_qkv": a_qkv, "a_gram": a_gram,
                          "a_exp": a_exp, "a_spread": a_spread, "f1_xn": norm("f1"), "f1_turn": turn("f1"),
                          "f1_up": up("f1"), "f2_xn": norm("f2"), "f2_turn": turn("f2"), "f2_up": up("f2"),
                          "b_xn": norm("b"), "b_turn": b_turn, "b_qkv": b_qkv, "b_softmax": b_softmax,
                          "b_turn_out": b_turn_out})

        @block.vector
        def _(dve):
            nc.vector.memset(mv[:, :, :, :], 0.0).then_inc(mv_zeros_ready, 1)
            nc.vector.memset(k_a[:, :, :, :], 0.0).then_inc(zeros_ready, 1)

            dve.wait_ge(bias_in, 16 * len(BIAS))
            steps = 0
            src = bias32
            for k in range(PARTS):
                last = nc.vector.tensor_copy(bias_part[:, k, :], src[:, :])
                if k < PARTS - 1:
                    last.then_inc(bias_steps, 1)
                    dve.wait_ge(bias_steps, steps + 1)
                    nc.vector.tensor_tensor(bias_rest[:, :], src[:, :], bias_part[:, k, :],
                                            ALU.subtract).then_inc(bias_steps, 1)
                    steps += 2
                    dve.wait_ge(bias_steps, steps)
                    src = bias_rest
            last.then_inc(bias_parts_ready, 1)

            def alone(eng):
                eng.wait_ge(zeros_ready, 1)

            def statistics(k, t):
                src = xw if k == "a" else xs[LN_IN[k]]
                if k != "a":
                    alone(dve)
                    wait(dve, x_ready[LN_IN[k]], t.n + 1)
                elif isinstance(t.n, int) and t.n in (0, n_early):
                    i = int(t.n > 0)
                    dve.wait_ge(xw_in[i], windows_loads[i])
                nc.vector.bn_stats(sums[k][:, t.half, :], src[:, t.n, :]).then_inc(ln_sums[k], 1)

            def aggregate(k, t):
                step = t.n + LN_LAG[k]
                wait(dve, ln_ready, step - 1)
                wait(dve, ln_sums[k], t.n + 1)
                i = LN.index(k)
                nc.vector.memset(wait_carrier[:, i:i + 1], 0.0)
                nc.vector.bn_aggr(mv[:, (t.half + LN_LAG[k]) % 2, i, :], sums[k][:, t.half, :]).then_inc(ln_mv[k], 1)

            def split_w_out():
                dve.wait_ge(w_in["a_out"], 16)
                dve.wait_ge(masks_ready, 1)
                nc.vector.tensor_tensor(wout_one[:, :, :], wout_a[:, :].unsqueeze(1).broadcast_to([P, HQ, C]),
                                        quad_mask[:, :, 0:1].broadcast_to([P, HQ, C]), ALU.mult
                                        ).then_inc(w_out_ready, 1)

            def add_residual(k, t, src, dst, psum):
                wait(dve, y_psum[k], t.n + 1)
                if k == "a" and isinstance(t.n, int) and t.n == 0:
                    dve.wait_ge(x_in, 16 * GROUPS)
                nc.vector.tensor_tensor(xs[dst][:, t.n, :], psum, xs[src][:, t.n, :], ALU.add
                                        ).then_inc(x_ready[dst], 1)

            def stats(k):
                return lambda t: statistics(k, t)

            def norm(k):
                return lambda t: aggregate(k, t)

            def a_logits(t):
                h = t.half
                wait(dve, gram_own_ready, t.n + 1)
                nc.vector.tensor_reduce(logit[:, :, :], gram_own[:, h].rearrange("p n h e -> p n e h"),
                                        AX_X, ALU.add).then_inc(logit_ready, 1)
                wait(dve, logit_ready, t.n + 1)
                nc.vector.tensor_reduce(logit_max[:, :], logit[:, :, :], AX_X, ALU.max
                                        ).then_inc(logit_max_ready, 1)
                wait(dve, logit_max_ready, t.n + 1)
                wait(dve, e_ready_a, t.n - 1)
                nc.vector.tensor_tensor(logit_low[:, h], logit[:, :, :],
                                        logit_max[:, :].unsqueeze(2).broadcast_to([P, NW, HD]),
                                        ALU.subtract).then_inc(logit_low_ready, 1)

            def a_sums(t):
                h = t.half
                wait(dve, e_ready_a, t.n + 1)
                nc.vector.tensor_reduce(e_sum_a[:, :], e_a[:, h], AX_X, ALU.add).then_inc(e_sum_ready_a, 1)
                wait(dve, e_sum_ready_a, t.n + 1)
                nc.vector.reciprocal(e_inv_a[:, h, :], e_sum_a[:, :]).then_inc(e_inv_ready_a, 1)

            def a_context(t):
                if isinstance(t.n, int) and t.n == 0:
                    split_w_out()
                wait(dve, o_psum, t.n + 1)
                wait(dve, e_inv_ready_a, t.n + 1)
                wait(dve, o_turned_ready, t.n - 1)
                nc.vector.tensor_tensor(
                    o_a[:, t.half].rearrange("p (j n) c -> p n j c", n=NW),
                    ps_out[:, 0:P].rearrange("p (n j c) -> p n j c", n=NW, j=GROUPS),
                    e_inv_a[:, t.half, :].unsqueeze(2).unsqueeze(3).broadcast_to([P, NW, GROUPS, HD]),
                    ALU.mult).then_inc(o_ready, 1)

            def a_turn_out(t):
                wait(dve, o_ready, t.n + 1)
                wait(dve, y_psum["a"], t.n - 1)
                nc.vector.transpose(o_turned[:, t.half].rearrange("p h m d -> p m h d"),
                                    o_a[:, t.half].unsqueeze(2).broadcast_to([P, NW * GROUPS, HQ, HD])
                                    ).then_inc(o_turned_ready, 1)

            def a_project(t):
                add_residual("a", t, 0, 1, ps_out[:, C:2 * C])

            def down(k):
                return lambda t: add_residual(k, t, *FFN[k], ps_f[k][:, 0:C])

            def b_qk(t):
                wait(dve, qkv_ready_b, t.n + 1)
                wait(dve, s_ready_own, t.n - 1)
                nc.vector.tensor_tensor(qk[:, t.half, OWN_QK], *q_times_k(t, OWN_QK), ALU.mult
                                        ).then_inc(qk_ready_own, 1)

            def b_s(heads, made, ready):
                def run(t):
                    wait(dve, made, t.n + 1)
                    nc.vector.tensor_reduce(s_b[:, heads, :], qk[:, t.half, heads], AX_X, ALU.add
                                            ).then_inc(ready, 1)
                return run

            def b_max(t):
                wait(dve, s_ready_own, t.n + 1)
                wait(dve, s_ready_pool, t.n + 1)
                nc.vector.tensor_reduce(s_max[:, :], s_b[:, :, :], AX_X, ALU.max).then_inc(s_max_ready, 1)

            def b_softmax(t):
                wait(dve, s_max_ready, t.n + 1)
                wait(dve, p_ready, t.n - 1)
                nc.vector.tensor_tensor(s_low[:, t.half], s_b[:, :, :],
                                        s_max[:, :].unsqueeze(2).broadcast_to([P, HEADS, HEADS]),
                                        ALU.subtract).then_inc(s_low_ready, 1)

            def b_pv(t):
                wait(dve, p_ready, t.n + 1)
                wait(dve, c_ready_own, t.n - 1)
                nc.vector.tensor_tensor(pv[:, t.half, OWN_PV], *v_times_p(t, OWN_PV), ALU.mult
                                        ).then_inc(pv_ready_own, 1)

            def b_sums(t):
                wait(dve, p_ready, t.n + 1)
                nc.vector.tensor_reduce(p_sum[:, :], p_b[:, t.half], AX_X, ALU.add).then_inc(p_sum_ready, 1)

            def b_c(heads, made, ready):
                def run(t):
                    wait(dve, made, t.n + 1)
                    nc.vector.tensor_reduce(c_raw[:, heads, :], pv[:, t.half, heads], AX_X, ALU.add
                                            ).then_inc(ready, 1)
                return run

            def b_inv(t):
                wait(dve, p_sum_ready, t.n + 1)
                nc.vector.reciprocal(p_inv[:, :], p_sum[:, :]).then_inc(p_inv_ready, 1)

            def b_scale(t):
                wait(dve, p_inv_ready, t.n + 1)
                wait(dve, c_ready_own, t.n + 1)
                wait(dve, c_ready_pool, t.n + 1)
                wait(dve, cT_psum, t.n - 1)
                nc.vector.tensor_tensor(c_b[:, t.half], c_raw[:, :, :],
                                        p_inv[:, :].unsqueeze(2).broadcast_to([P, HEADS, HD]),
                                        ALU.mult).then_inc(c_ready, 1)

            def b_project(t):
                add_residual("b", t, 2, 3, ps_b_out[:, 0:C])

            walk(dve, T, {"a_norm": norm("a"), "a_logits": a_logits, "a_sums": a_sums,
                          "a_context": a_context, "a_turn_out": a_turn_out, "a_project": a_project,
                          "f1_norm": norm("f1"), "f1_down": down("f1"), "f2_norm": norm("f2"),
                          "f2_down": down("f2"), "b_norm": norm("b"), "b_project": b_project,
                          "a_stats": stats("a"), "f1_stats": stats("f1"), "b_stats": stats("b"),
                          "f2_stats": stats("f2"),
                          "b_qk": b_qk, "b_s_own": b_s(OWN_QK, qk_ready_own, s_ready_own),
                          "b_s_pool": b_s(POOL_QK, qk_ready_pool, s_ready_pool), "b_max": b_max,
                          "b_softmax": b_softmax, "b_sums": b_sums, "b_inv": b_inv, "b_pv": b_pv,
                          "b_c_own": b_c(OWN_PV, pv_ready_own, c_ready_own),
                          "b_c_pool": b_c(POOL_PV, pv_ready_pool, c_ready_pool), "b_scale": b_scale})

        @block.tensor
        def _(pe):
            pe.wait_ge(ident_ready, 1)
            pe.wait_ge(ones_ready, 1)

            def mm(psum, lhsT, rhs, start=False, stop=False):
                return nc.tensor.matmul(psum, lhsT, rhs, start=start, stop=stop)

            def turn_in(k, t, psum):
                wait(pe, xn_ready[k], t.n + 1)
                nc.tensor.transpose(psum, xn[k][:, t.half, :], ident[:, :]).then_inc(xnT_psum[k], 1)

            def first(t):
                return isinstance(t.n, int) and t.n == 0

            def a_turn(t):
                wait(pe, v_ready_a, t.n)
                turn_in("a", t, ps_in[:, 3 * C:4 * C])

            def a_qkv(t):
                wait(pe, xnT_ready["a"], t.n + 1)
                if first(t):
                    pe.wait_ge(w_in["a_qkv"], 16)
                    pe.wait_ge(bias_ready, 16 * 2 * PARTS)
                xT = xnT["a"][:, t.half, :]
                b = bias[:, bias_at["a_qkv"]]
                mm(ps_in[:, 0:2 * C], xT, wqkv_a[:, 0:2 * C], start=True)
                mm(ps_in[:, 0:2 * C], ones[:, :], b[:, 0:2 * C], stop=True)
                mm(ps_in[:, 2 * C:3 * C], wqkv_a[:, 2 * C:3 * C], xT, start=True)
                mm(ps_in[:, 2 * C:3 * C], b[:, 2 * C:3 * C], ones[:, :], stop=True).then_inc(qkv_psum_a, 1)

            def a_gram(t):
                wait(pe, qk_ready_a, t.n + 1)
                wait(pe, gram_ready, t.n)
                mm(ps_gram[:, :], q_a[:, t.half, :], k_a[:, t.half].rearrange("p n c -> p (n c)"),
                   start=True, stop=True).then_inc(gram_psum, 1)

            def a_spread(t):
                wait(pe, e_diag_ready, t.n + 1)
                wait(pe, eT_ready, t.n)
                for n in range(NW):
                    last = nc.tensor.transpose(ps_eT[:, P * n:P * (n + 1)],
                                               e_diag[:, t.half, n].rearrange("p h e -> p (h e)"), ident[:, :])
                last.then_inc(eT_psum, 1)

            def a_context(t):
                wait(pe, eT_ready, t.n + 1)
                wait(pe, v_ready_a, t.n + 1)
                wait(pe, x_ready[1], t.n)
                for n in range(NW):
                    cols = slice(WIN * n, WIN * (n + 1))
                    last = mm(ps_out[:, cols], eT[:, t.half, n, :], vT_a[:, t.half, cols], start=True, stop=True)
                last.then_inc(o_psum, 1)

            def a_project(t):
                wait(pe, o_turned_ready, t.n + 1)
                wait(pe, o_ready, t.n + 1)
                if first(t):
                    pe.wait_ge(w_out_ready, 1)
                for i in range(HQ):
                    mm(ps_out[:, C:2 * C], o_turned[:, t.half, i].rearrange("p m d -> p (m d)"),
                       wout_one[:, i, :], start=i == 0)
                mm(ps_out[:, C:2 * C], ones[:, :], bias[:, bias_at["a_out"]], stop=True
                   ).then_inc(y_psum["a"], 1)

            def turn(k):
                def run(t):
                    wait(pe, x_ready[FFN[k][1]], t.n)
                    turn_in(k, t, ps_f[k][:, 0:P])
                return run

            def up(k):
                def run(t):
                    if first(t):
                        pe.wait_ge(w_in["f"], 32)
                        pe.wait_ge(chunks_ready, 1 + PARTS)
                    wait(pe, xnT_ready[k], t.n + 1)
                    mm(ps_f[k][:, :], bias_up[:, :], chunk_of[:, :, :].rearrange("r i n -> r (i n)"), start=True)
                    for i in range(NF):
                        cols = slice(P * i, P * (i + 1))
                        last = mm(ps_f[k][:, cols], w1[:, cols], xnT[k][:, t.half, :], stop=i == NF - 1)
                    last.then_inc(h_psum[k], 1)
                return run

            def down(k):
                def run(t):
                    wait(pe, h_ready[k], t.n + 1)
                    for i in range(NF):
                        mm(ps_f[k][:, 0:C], hT[k][:, t.half, i, :], w2[:, i, :], start=i == 0)
                    mm(ps_f[k][:, 0:C], ones[:, :], bias[:, bias_at["f2"]], stop=True).then_inc(y_psum[k], 1)
                return run

            def b_turn(t):
                wait(pe, qkv_ready_b, t.n)
                turn_in("b", t, ps_b_in[:, 3 * C:4 * C])

            def b_qkv(t):
                if first(t):
                    pe.wait_ge(w_in["b"], 32)
                wait(pe, xnT_ready["b"], t.n + 1)
                mm(ps_b_in[:, 0:3 * C], xnT["b"][:, t.half, :], wqkv_b[:, :], start=True)
                mm(ps_b_in[:, 0:3 * C], ones[:, :], bias[:, bias_at["b_qkv"]], stop=True
                   ).then_inc(qkv_psum_b, 1)

            def b_turn_out(t):
                wait(pe, c_ready, t.n + 1)
                wait(pe, x_ready[3], t.n)
                nc.tensor.transpose(ps_b_out[:, C:2 * C], c_b[:, t.half].rearrange("p h d -> p (h d)"),
                                    ident[:, :]).then_inc(cT_psum, 1)

            def b_project(t):
                wait(pe, cT_ready, t.n + 1)
                mm(ps_b_out[:, 0:C], cT_b[:, t.half, :], wout_b[:, :], start=True)
                mm(ps_b_out[:, 0:C], ones[:, :], bias[:, bias_at["b_out"]], stop=True).then_inc(y_psum["b"], 1)

            walk(pe, T, {"a_turn": a_turn, "a_qkv": a_qkv, "a_gram": a_gram, "a_spread": a_spread,
                         "a_context": a_context, "a_project": a_project, "f1_turn": turn("f1"),
                         "f1_up": up("f1"), "f1_down": down("f1"), "f2_turn": turn("f2"), "f2_up": up("f2"),
                         "f2_down": down("f2"), "b_turn": b_turn, "b_qkv": b_qkv,
                         "b_turn_out": b_turn_out, "b_project": b_project})


_INS = ["L0_attn_a_x", "L0_attn_a_W_qkv", "L0_attn_a_b_qkv", "L0_attn_a_W_out", "L0_attn_a_b_out",
        "L0_attn_b_W_qkv", "L0_attn_b_b_qkv", "L0_attn_b_W_out", "L0_attn_b_b_out",
        "L0_ffn_w1", "L0_ffn_b1", "L0_ffn_w2", "L0_ffn_b2"]


def kernel(**inputs):
    import numpy as _np
    import concourse.bacc as _bacc
    from concourse import mybir as _mybir
    from concourse.bass_utils import run_bass_kernel_spmd as _run

    nc = _bacc.Bacc("TRN2", target_bir_lowering=False, num_devices=1)
    arrays, args = {}, []
    for name in _INS:
        a = _np.ascontiguousarray(inputs[name])
        arrays[f"in_{name}_dram"] = a
        args.append(nc.dram_tensor(f"in_{name}_dram", a.shape, _mybir.dt.from_np(a.dtype),
                                   kind="ExternalInput").ap())
    shape = inputs["L0_attn_a_x"].shape
    args.append(nc.dram_tensor("out_0_dram", shape, _mybir.dt.float32, kind="ExternalOutput").ap())
    hybrid_block(nc, *args)
    r = _run(nc, [arrays], core_ids=[0])
    return r.results[0]["out_0_dram"]
```
